# Optimizing a Trainium2 kernel written in Bass

```python
import numpy as np
import jax
import jax.numpy as jnp

def _softmax(x, axis=-1):
    return jax.nn.softmax(x, axis=axis)

def _gelu(x):
    return jax.nn.gelu(x, approximate=True)

def _silu(x):
    return jax.nn.silu(x)

def _sigmoid(x):
    return jax.nn.sigmoid(x)

def _layernorm(x, axis=-1, eps=1e-05):
    m = jnp.mean(x, axis=axis, keepdims=True)
    v = jnp.var(x, axis=axis, keepdims=True)
    return (x - m) / jnp.sqrt(v + eps)

def _scatter_add(tgt, idx, src, axis=0):
    return tgt.at[idx].add(src)

def _segment_sum(src, seg, n):
    return jax.ops.segment_sum(src, seg, n)
kernel_name = 'mk_seq_preln_d1_jaxref_r8_60f580'

def setup_inputs(seed: int=0):
    np.random.seed(seed)
    _w = jnp.asarray

    def _L0_attn_setup():
        import jax, jax.numpy as jnp
        import numpy as np
        DIM = 128
        H = 16
        HD = DIM // H
        BS = 64
        SPARSITY = 0.95
        SCALE = HD ** (-0.5)
        key = jax.random.key(seed)
        k1, k2, k3 = jax.random.split(key, 3)
        B, N = (2, 256)
        x = jax.random.normal(k1, (B, N, DIM), jnp.float32)
        qkv_w = jax.random.normal(k2, (3 * DIM, DIM), jnp.float32) * DIM ** (-0.5)
        proj_w = jax.random.normal(k3, (DIM, DIM), jnp.float32) * DIM ** (-0.5)
        proj_b = jnp.zeros((DIM,), jnp.float32)
        return {'x': x, 'qkv_w': qkv_w, 'proj_w': proj_w, 'proj_b': proj_b}
    _L0_attn_in = _L0_attn_setup()

    def _L0_ffn_setup():
        import jax, jax.numpy as jnp
        import numpy as np
        B, S, D, H, E, K = (4, 256, 128, 512, 4, 2)
        key = jax.random.key(seed)
        ks = jax.random.split(key, 7)
        s1 = 1.0 / np.sqrt(D)
        s2 = 1.0 / np.sqrt(H)
        return {'x': jax.random.normal(ks[0], (B, S, D), jnp.float32), 'w1': jax.random.uniform(ks[1], (E, D, H), jnp.float32, -s1, s1), 'b1': jax.random.uniform(ks[2], (E, H), jnp.float32, -s1, s1), 'w2': jax.random.uniform(ks[3], (E, H, D), jnp.float32, -s2, s2), 'b2': jax.random.uniform(ks[4], (E, D), jnp.float32, -s2, s2), 'wr': jax.random.uniform(ks[5], (D, E), jnp.float32, -s1, s1), 'br': jax.random.uniform(ks[6], (E,), jnp.float32, -s1, s1)}
    _L0_ffn_in = _L0_ffn_setup()
    _d = {'L0_attn_x': _L0_attn_in['x'], 'L0_attn_qkv_w': _L0_attn_in['qkv_w'], 'L0_attn_proj_w': _L0_attn_in['proj_w'], 'L0_attn_proj_b': _L0_attn_in['proj_b'], 'L0_ffn_w1': _L0_ffn_in['w1'], 'L0_ffn_b1': _L0_ffn_in['b1'], 'L0_ffn_w2': _L0_ffn_in['w2'], 'L0_ffn_b2': _L0_ffn_in['b2'], 'L0_ffn_wr': _L0_ffn_in['wr'], 'L0_ffn_br': _L0_ffn_in['br']}
    _x0 = _d['L0_attn_x']
    _d['L0_attn_x'] = jax.random.normal(jax.random.fold_in(jax.random.key(seed), 1), (16, 512, 128), dtype=_x0.dtype)
    del _x0
    return _d

def reference(L0_attn_x, L0_attn_qkv_w, L0_attn_proj_w, L0_attn_proj_b, L0_ffn_w1, L0_ffn_b1, L0_ffn_w2, L0_ffn_b2, L0_ffn_wr, L0_ffn_br):

    def _L0_attn_ref(x, qkv_w, proj_w, proj_b):
        import jax, jax.numpy as jnp
        import numpy as np
        DIM = 128
        H = 16
        HD = DIM // H
        BS = 64
        SPARSITY = 0.95
        SCALE = HD ** (-0.5)
        B, N, D = x.shape
        qkv = (x @ qkv_w.T).reshape(B, N, 3, H, HD).transpose(2, 0, 3, 1, 4)
        q, k, v = (qkv[0], qkv[1], qkv[2])
        M = N // BS
        qb = q.reshape(B, H, M, BS, HD).mean(axis=3)
        kb = k.reshape(B, H, M, BS, HD).mean(axis=3)
        c = jnp.einsum('bhmd,bhnd->bhmn', qb, kb) * SCALE
        k_keep = max(1, int(round(M * (1.0 - SPARSITY))))
        thresh = jax.lax.top_k(c, k_keep)[0][..., -1:]
        block_mask = (c >= thresh) | jnp.eye(M, dtype=bool)
        tmask = jnp.repeat(jnp.repeat(block_mask, BS, axis=2), BS, axis=3)
        scores = jnp.einsum('bhqd,bhkd->bhqk', q, k) * SCALE
        scores = jnp.where(tmask, scores, -jnp.inf)
        probs = jax.nn.softmax(scores, axis=-1)
        out = jnp.einsum('bhqk,bhkd->bhqd', probs, v)
        out = out.transpose(0, 2, 1, 3).reshape(B, N, D)
        return out @ proj_w.T + proj_b

    def _L0_ffn_ref(x, w1, b1, w2, b2, wr, br):
        import jax, jax.numpy as jnp
        import numpy as np
        B, S, D, H, E, K = (4, 256, 128, 512, 4, 2)
        Bx, Sx, Dx = x.shape
        xf = x.reshape(-1, Dx)
        logits = xf @ wr + br
        topk_vals, topk_idx = jax.lax.top_k(logits, K)
        gates = jax.nn.softmax(topk_vals, axis=-1)
        h = jax.nn.gelu(jnp.einsum('nd,edh->enh', xf, w1) + b1[:, None, :], approximate=False)
        y = jnp.einsum('enh,ehd->end', h, w2) + b2[:, None, :]
        c = jnp.einsum('eh,ehd->ed', jax.nn.gelu(b1, approximate=False), w2) + b2
        c_sum = c.sum(axis=0)
        yt = jnp.transpose(y, (1, 0, 2))
        y_sel = jnp.take_along_axis(yt, topk_idx[:, :, None], axis=1)
        c_sel = c[topk_idx]
        out = jnp.einsum('nk,nkd->nd', gates, y_sel - c_sel + c_sum[None, None, :])
        return out.reshape(Bx, Sx, Dx)
    x = L0_attn_x
    x = x + _L0_attn_ref(_layernorm(x, axis=-1), L0_attn_qkv_w, L0_attn_proj_w, L0_attn_proj_b)
    x = x + _L0_ffn_ref(_layernorm(x, axis=-1), L0_ffn_w1, L0_ffn_b1, L0_ffn_w2, L0_ffn_b2, L0_ffn_wr, L0_ffn_br)
    return x

_drawn_inputs = setup_inputs


def setup_inputs(seed=0):
    import zlib

    import numpy as np

    out = dict(_drawn_inputs(seed))
    spreads = {'L0_attn_proj_b': (0.0, 0.1)}
    factors = {}
    for name, (base, spread) in spreads.items():
        noise = np.random.default_rng([zlib.crc32(name.encode()), seed]).standard_normal(out[name].shape)
        drawn = base * np.exp(spread * noise) if base else spread * noise
        out[name] = jnp.asarray(drawn.astype(out[name].dtype))
    for name, factor in factors.items():
        out[name] = (out[name] * factor).astype(out[name].dtype)
    return out
```

```python
from contextlib import ExitStack

import numpy as np

import concourse.bass as bass
from concourse import mybir

F32 = mybir.dt.float32
F32R = mybir.dt.float32r
BF16 = mybir.dt.bfloat16
U32 = mybir.dt.uint32
ALU = mybir.AluOpType
ACT = mybir.ActivationFunctionType
AXX = mybir.AxisListType.X

P = 128
B, N, D = 16, 512, 128
H = 16
HD = D // H
BS = 64
M = N // BS
T = N // P
SCALE = HD ** -0.5
EPS = 1e-5
E, HID = 4, 512
C = HID // P
QUADS = 4
HQ = H // QUADS
KEYS = 2 * BS
ROW = 3 * BS
FAR = 1e30
VW = 32


class Event:

    def __init__(self, sem, step=1):
        self.sem, self.step, self.count = sem, step, 0

    def tick(self):
        self.count += self.step
        return self.sem, self.count


class Run:

    def __init__(self, event, name):
        self.dve, self.pool, self.act, self.pe = (event(f"{name}_{e}") for e in ("dve", "pool", "act", "pe"))
        self.lists = {e: [] for e in ("sync", "gpsimd", "scalar", "vector", "tensor")}
        self.waited = {e: {} for e in self.lists}

    def put(self, engine, emit, after=(), done=None):
        waits = []
        for token in after:
            if token is None:
                continue
            sem, value = token
            if self.waited[engine].get(id(sem), 0) < value:
                self.waited[engine][id(sem)] = value
                waits.append(token)
        token = done.tick() if done else None
        self.lists[engine].append((waits, emit, done))
        return token

    def block(self, nc):
        with nc.Block() as block:
            block.sync(lambda eng: self.play("sync", eng))
            block.gpsimd(lambda eng: self.play("gpsimd", eng))
            block.scalar(lambda eng: self.play("scalar", eng))
            block.vector(lambda eng: self.play("vector", eng))
            block.tensor(lambda eng: self.play("tensor", eng))

    def play(self, engine, eng):
        for waits, emit, done in self.lists[engine]:
            for sem, value in waits:
                eng.wait_ge(sem, value)
            ins = emit(eng)
            if done:
                ins.then_inc(done.sem, done.step)


def layer(nc, x, wqkv_t, wproj_t, proj_b, w1, b1_t, w2, b2, wr, br, ident, quad_mask, head_sum,
          head_one, block_rank, row_base, expert_rows, own_block, head_mask,
          query_rows, key_rows, out):
    with ExitStack() as ctx:
        def sb(name, shape, dt=F32):
            return ctx.enter_context(nc.sbuf_tensor(name, shape, dt))

        def ps(name, shape, dt=F32):
            return ctx.enter_context(nc.psum_tensor(name, shape, dt))

        def ev(name, step=1):
            return Event(ctx.enter_context(nc.semaphore(name)), step)

        wqkv = sb("wqkv", [P, 3 * D])
        wproj = sb("wproj", [P, D])
        projb = sb("projb", [P, D])
        w1s = sb("w1s", [P, E, HID])
        w2s = sb("w2s", [P, E * C, D])
        b1s = sb("b1s", [P, E * C])
        b2s = sb("b2s", [E, D])
        wrs = sb("wrs", [P, E])
        brs = sb("brs", [P, E])
        idn = sb("idn", [P, P])
        qmask = sb("qmask", [P, HQ])
        hsum = sb("hsum", [P, P])
        hone32 = sb("hone32", [H, H, P])
        hone = sb("hone", [H, H, P], BF16)
        rank = sb("rank", [P, M, M])
        rbase = sb("rbase", [P, 1])
        erows = sb("erows", [P, E, C, E])
        neg_half = sb("neg_half", [P, T])
        ones4 = sb("ones4", [E, E])
        g1 = sb("g1", [P, E, C])
        g1m = sb("g1m", [P, E, C, E])
        cexp = sb("cexp", [E, D])
        mexp = sb("mexp", [E, D])

        NX = 3
        xs = [sb(f"xs{i}", [P, T, D]) for i in range(NX)]
        xpb = [sb(f"xpb{i}", [P, T, D]) for i in range(NX)]
        x2 = [sb(f"x2{i}", [P, T, D]) for i in range(NX)]
        stats = sb("stats", [P, T, 6])
        mv = sb("mv", [P, T, 2])
        veps = sb("veps", [P, T])
        rstd = sb("rstd", [P, T])
        xn = sb("xn", [P, T, D])
        xnT = sb("xnT", [P, N])
        qhi = sb("qhi", [P, N], F32R)
        qlo = sb("qlo", [P, N])
        qmh = [sb(f"qmh{i}", [P, HQ, N], F32R) for i in range(2)]
        qml = [sb(f"qml{i}", [P, HQ, N], F32R) for i in range(2)]
        stage = [sb(f"stage{i}", [P, M, BS, 3], F32R) for i in range(2)]
        kv = [sb(f"kv{i}", [P, M, KEYS, 3], F32R) for i in range(2)]
        qsum = sb("qsum", [P, M])
        ksum = sb("ksum", [P, M])
        qk = sb("qk", [P, M, M])
        crow = sb("crow", [P, M, M])
        cmax = sb("cmax", [P, M])
        ceq = sb("ceq", [P, M, M])
        crank = sb("crank", [P, M, M])
        cbest = sb("cbest", [P, M])
        index = [sb(f"index{i}", [P, M], U32) for i in range(2)]
        ties = sb("ties", [P, B, M])
        vaug = [sb(f"vaug{i}", [P, H, VW]) for i in range(2)]
        rmax = [sb(f"rmax{i}", [P, H, 2]) for i in range(2)]
        nmax = [sb(f"nmax{i}", [H, BS], BF16) for i in range(2)]
        prob = [sb(f"prob{i}", [P, H, BS]) for i in range(2)]
        oT = sb("oT", [P, HQ, P])
        rden = sb("rden", [P, H])
        att = sb("att", [P, H, HD])
        attT = sb("attT", [P, P])
        stats2 = sb("stats2", [P, T, 6])
        mv2 = sb("mv2", [P, T, 2])
        veps2 = sb("veps2", [P, T])
        rstd2 = sb("rstd2", [P, T])
        xn2 = sb("xn2", [P, T, D])
        tiemax, tieall = sb("tiemax", [P, 1]), sb("tieall", [1, 1])
        tieflag = sb("tieflag", [1, 1], U32)
        own = sb("own", [P, M, M])
        hmask = sb("hmask", [P, H])
        qrows = sb("qrows", [M * M, N])
        krows = sb("krows", [M * M, N])
        gq, gk, gqh = sb("gq", [P, N]), sb("gk", [P, N]), sb("gqh", [P, N])
        gv, gatt = sb("gv", [P, T, D]), sb("gatt", [P, T, D])
        gbias, gbh = sb("gbias", [M * M, P]), sb("gbh", [M * M, N])
        gp, gpT = sb("gp", [P, N]), sb("gpT", [P, N])
        gmax, gsumr = sb("gmax", [P, 1]), sb("gsumr", [P, 1])
        xn2T = sb("xn2T", [P, N])
        logit = sb("logit", [P, T, E])
        beats = sb("beats", [P, T, E])
        pair = sb("pair", [P, T, E])
        nbeats = sb("nbeats", [P, T, E])
        lmax = sb("lmax", [P, T])
        gexp = sb("gexp", [P, T, E])
        gsum = sb("gsum", [P, T])
        gate = sb("gate", [P, T, E])
        gateT = sb("gateT", [E, N])
        hid = [sb(f"hid{i}", [P, C, N]) for i in range(2)]

        table = [nc.dram_tensor(f"kv_table{b}", [P * M, ROW], F32, kind="Internal").ap() for b in range(B)]

        s_ps = [ps(f"s_ps{i}", [P, 2 * N]) for i in range(2)]
        o_ps = ps("o_ps", [P, HQ, P])
        v_ps = ps("v_ps", [P, N])
        a_ps = ps("a_ps", [P, N])
        c_ps = ps("c_ps", [P, N])

        weights_in = ev("weights_in", 16)
        x_in = [ev(f"x_in{i}", 16) for i in range(NX)]
        table_out = [ev(f"table_out{i}", 16) for i in range(2)]
        own_in = [ev(f"own_in{i}", 16) for i in range(2)]
        sel_in = [ev(f"sel_in{i}", 16) for i in range(2)]
        out_done = [ev(f"out_done{i}", 16) for i in range(NX)]
        run = Run(ev, "fast")

        def V(emit, *after):
            return run.put("vector", emit, after, run.dve)

        def G(emit, *after):
            return run.put("gpsimd", emit, after, run.pool)

        def A(emit, *after):
            return run.put("scalar", emit, after, run.act)

        def PEq(emits, *after):
            for n, emit in enumerate(emits):
                token = run.put("tensor", emit, after if n == 0 else (), run.pe if n == len(emits) - 1 else None)
            return token

        loads = [(idn, ident), (wqkv, wqkv_t), (qmask, quad_mask), (hsum, head_sum), (rank, block_rank),
                 (rbase, row_base), (wproj, wproj_t), (hone32, head_one),
                 (projb, proj_b),
                 (w1s, w1.rearrange("e d h -> d e h")), (w2s, w2.rearrange("e (c p) d -> p (e c) d", p=P)),
                 (b1s, b1_t), (b2s, b2), (wrs, wr), (brs, br), (erows, expert_rows), (own, own_block),
                 (hmask, head_mask), (qrows, query_rows), (krows, key_rows)]
        tok_x, tok_x2, tok_xpb = {}, {}, {}
        tok_ffn_done, tok_store = {}, {}

        def load_x(b):
            i = b % NX
            tok_x[b] = run.put("sync", lambda e: e.dma_start(
                xs[i][:], x[b].rearrange("(t p) d -> p t d", p=P)),
                [tok_xpb.get(b - NX), tok_xn.get(b - NX)], x_in[i])

        tok_xn = {}
        load_x(0)
        for dst, src in loads:
            w_in = run.put("sync", lambda e, dst=dst, src=src: e.dma_start(dst[:], src), (), weights_in)
        load_x(1)

        c0 = V(lambda e: e.memset(neg_half[:], -0.5))
        V(lambda e: e.memset(ones4[:], 1.0))
        for i in range(2):
            V(lambda e, i=i: e.memset(vaug[i][:], 0.0))
        for i in range(2):
            c1 = V(lambda e, i=i: e.memset(vaug[i][:, :, HD:HD + 1], 1.0), (run.dve.sem, run.dve.count))

        tok_hone = V(lambda e: e.tensor_copy(hone[:], hone32[:]), w_in)

        t = A(lambda e: e.activation(g1[:], b1s[:].rearrange("p (e c) -> p e c", e=E), ACT.Gelu), w_in)
        t = V(lambda e: e.tensor_tensor(g1m[:], erows[:], g1[:].rearrange("p e (c o) -> p e c o", o=1).broadcast_to([P, E, C, E]), ALU.mult), t, w_in)
        t = PEq([lambda e, k=k: e.matmul(a_ps[0:E, 0:D], g1m[:, k // C, k % C, :], w2s[:, k, :],
                                         start=(k == 0), stop=(k == E * C - 1)) for k in range(E * C)], t)
        t = V(lambda e: e.tensor_tensor(cexp[:], a_ps[0:E, 0:D], b2s[:], ALU.add), t)
        t = PEq([lambda e: e.matmul(a_ps[0:E, 0:D], ones4[:], cexp[:], start=True, stop=True)], t)
        t = V(lambda e: e.tensor_tensor(mexp[:], a_ps[0:E, 0:D], cexp[:], ALU.subtract), t)
        tok_mexp = V(lambda e: e.tensor_tensor(mexp[:], mexp[:], b2s[:], ALU.add), t)

        free = {"a": tok_mexp, "v": None, "c": None, "o": None, "s": [None, None]}
        last = {}

        def norm_stats(src, st, m_v, ve, rs, tok_src):
            for k in range(T):
                t = V(lambda e, k=k: e.bn_stats(st[:, k, :], src[:, k, :]), tok_src)
            for k in range(T):
                t2 = V(lambda e, k=k: e.bn_aggr(m_v[:, k, :], st[:, k, :]), t)
            t = G(lambda e: e.tensor_scalar(ve[:], m_v[:, :, 1], EPS, None, ALU.add), t2)
            return G(lambda e: e.tensor_tensor(rs[:], ve[:], neg_half[:], ALU.pow), t, c0)

        def norm_rows(src, m_v, rs, dst, tok, free_dst):
            for k in range(T):
                t = V(lambda e, k=k: e.tensor_scalar(dst[:, k, :], src[:, k, :], m_v[:, k, 0:1],
                                                     rs[:, k:k + 1], ALU.subtract, ALU.mult), tok, free_dst)
            return t

        def rows_to_columns(src, dst, tok, free_dst):
            t = PEq([lambda e, k=k: e.transpose(a_ps[:, k * P:(k + 1) * P], src[:, k, :], idn[:])
                     for k in range(T)], tok, free["a"], w_in)
            free["a"] = A(lambda e: e.copy(dst[:], a_ps[:]), t, free_dst)
            return t, free["a"]

        sA = {}

        def a_norm(b):
            i = b % NX
            t = norm_stats(xs[i], stats, mv, veps, rstd, tok_x[b])
            tok_xpb[b] = G(lambda e: e.tensor_tensor(
                xpb[i][:], xs[i][:], projb[:].rearrange("p (o d) -> p o d", o=1).broadcast_to([P, T, D]), ALU.add),
                tok_x[b], w_in, last.get(("x2", b - NX)))
            t = norm_rows(xs[i], mv, rstd, xn, t, last.get("xn_read"))
            tok_xn[b] = t
            last["xn_read"], sA["xnT"] = rows_to_columns(xn, xnT, t, last.get("xnT_read"))

        def project(part, b):
            t = PEq([lambda e: e.matmul(a_ps[:], wqkv[:, part * D:(part + 1) * D], xnT[:],
                                        start=True, stop=True)], sA["xnT"], free["a"], w_in)
            last["xnT_read"] = t
            return t

        def a_q(b):
            j = b % 2
            t = project(0, b)
            hi = V(lambda e: e.tensor_copy(qhi[:], a_ps[:]), t, last.get("qhi_read"))
            V(lambda e: e.tensor_reduce(qsum[:], a_ps[:].rearrange("p (m s) -> p m s", s=BS), AXX, ALU.add), t)
            lo = V(lambda e: e.tensor_tensor(qlo[:], a_ps[:], qhi[:].bitcast(F32), ALU.subtract), hi)
            free["a"] = lo
            for h in range(HQ):
                t = V(lambda e, h=h: e.tensor_scalar(qmh[j][:, h, :], qhi[:].bitcast(F32), qmask[:, h:h + 1],
                                                     None, ALU.mult), hi, w_in, last.get(("q_read", j)))
            for h in range(HQ):
                u = G(lambda e, h=h: e.tensor_scalar(qml[j][:, h, :], qlo[:], qmask[:, h:h + 1],
                                                     None, ALU.mult), lo, w_in, last.get(("q_read", j)))
            last["qhi_read"] = u
            sA[("q", b)] = (t, u)

        def a_k(b):
            j = b % 2
            t = project(1, b)
            st = stage[j]
            kview = a_ps[:].rearrange("p (m s) -> p m s", s=BS)
            hi = V(lambda e: e.tensor_copy(st[:, :, :, 0], kview), t, last.get(("stage_read", j)), last.get(("stage_read2", j)))
            V(lambda e: e.tensor_reduce(ksum[:], kview, AXX, ALU.add), t)
            free["a"] = V(lambda e: e.tensor_tensor(st[:, :, :, 1], kview, st[:, :, :, 0].bitcast(F32),
                                                    ALU.subtract), hi)
            sA["k"] = free["a"]
            sA["qk"] = V(lambda e: e.tensor_tensor(
                qk[:], qsum[:].rearrange("p (m o) -> p m o", o=1).broadcast_to([P, M, M]),
                ksum[:].rearrange("p (o n) -> p o n", o=1).broadcast_to([P, M, M]), ALU.mult), free["a"])

        def a_v(b):
            j = b % 2
            st = stage[j]
            t = project(2, b)
            free["a"] = A(lambda e: e.copy(st[:, :, :, 2].bitcast(F32), a_ps[:].rearrange("p (m s) -> p m s", s=BS)),
                          t, last.get(("stage_read", j)), last.get(("stage_read2", j)))
            tb = run.put("sync", lambda e: e.dma_start(
                table[b][:, :].rearrange("(p n) c -> p (n c)", n=M), st[:].bitcast(F32).rearrange("p n s c -> p (n s c)")),
                [free["a"], sA["k"]], table_out[j])
            own = run.put("sync", lambda e: e.dma_start(kv[j][:, :, 0:BS, :].bitcast(F32).rearrange("p m s c -> p m (s c)"), st[:].bitcast(F32).rearrange("p m s c -> p m (s c)")),
                        [last.get(("kv_read", j))], own_in[j])
            last[("stage_read", j)], last[("stage_read2", j)] = tb, own
            sA[("own", b)] = own
            sA["table"] = tb

        def products():
            t = PEq([lambda e: e.matmul(a_ps[:, 0:M * M], hsum[:], qk[:].rearrange("p m n -> p (m n)"),
                                        start=True, stop=True)], sA["qk"], free["a"], w_in)
            t = V(lambda e: e.tensor_scalar(crow[:].rearrange("p m n -> p (m n)"), a_ps[:, 0:M * M],
                                            1.0 / (BS * BS), SCALE, ALU.mult, ALU.mult), t)
            free["a"] = t
            t = V(lambda e: e.tensor_reduce(cmax[:], crow[:], AXX, ALU.max), t)
            return V(lambda e: e.tensor_tensor(ceq[:], crow[:], cmax[:].rearrange("p (m o) -> p m o", o=1).broadcast_to([P, M, M]),
                                               ALU.is_ge), t)

        def a_select(b):
            j = b % 2
            t = products()
            last["ties"] = V(lambda e: e.tensor_reduce(ties[:, b, :], ceq[:], AXX, ALU.add), t)
            t = V(lambda e: e.tensor_tensor(crank[:], ceq[:], rank[:], ALU.mult), t, w_in)
            t = V(lambda e: e.tensor_reduce(cbest[:], crank[:], AXX, ALU.max), t)
            t = V(lambda e: e.tensor_scalar(index[j][:], cbest[:], -1.0, rbase[:], ALU.mult, ALU.add), t,
                  last.get(("index_read", j)))
            for m in range(M):
                g = run.put("gpsimd", lambda e, m=m: e.indirect_dma_start(
                    out=kv[j][:, m, BS:, :].bitcast(F32).rearrange("p s c -> p (s c)"), out_offset=None, in_=table[b][:, :],
                    in_offset=bass.IndirectOffsetOnAxis(ap=index[j][:, m:m + 1], axis=0)),
                    [t, sA["table"], last.get(("kv_read", j))], sel_in[j])
            last[("index_read", j)] = g
            sA[("sel", b)] = g

        tB = {}

        def scores(b, m):
            j, i = b % 2, m % 2
            keys_hi = kv[j][:, m, :, 0]
            keys_lo = kv[j][:, m, :, 1]
            halves = []
            for g, bank_first in ((0, True), (2, True), (1, False), (3, False)):
                r = slice(32 * g, 32 * g + 32)
                dst = s_ps[i][:, g * HQ * BS:(g + 1) * HQ * BS].rearrange("p (h s) -> p h s", s=BS)
                qh = qmh[j][r, :, m * BS:(m + 1) * BS]
                ql = qml[j][r, :, m * BS:(m + 1) * BS]
                emits = [lambda e, l=l, rr=rr, s=s, dst=dst: e.matmul(dst, l, rr, start=s, stop=False, skip_group_check=True)
                         for l, rr, s in ((keys_hi[r], qh, bank_first), (keys_hi[r], ql, False), (keys_lo[r], qh, False))]
                halves.append(PEq(emits, halves[-2] if len(halves) >= 2 else None, *sA[("q", b)], sA[("own", b)], sA[("sel", b)], free["s"][i]))
            tB[("s", b, m)] = halves[2], halves[3]

        def values(b, m):
            j, i = b % 2, m % 2
            t = PEq([lambda e: e.transpose(v_ps[:, 0:P], kv[j][:, m, :, 2].bitcast(F32), idn[:])],
                    sA[("own", b)], sA[("sel", b)], free["v"])
            last[("kv_read", j)] = t
            t = A(lambda e: e.copy(vaug[i][:, :, 0:HD], v_ps[:, 0:P].rearrange("p (h d) -> p h d", d=HD)), t, c1,
                  last.get(("vaug_read", i)))
            free["v"] = t
            tB[("v", b, m)] = t

        def block_max(b, m):
            i = m % 2
            for half in range(2):
                t = V(lambda e, half=half: e.tensor_reduce(
                    rmax[i][:, half * 8:(half + 1) * 8, :],
                    s_ps[i][:, half * N:(half + 1) * N].rearrange("p (a c) -> p a c", c=32), AXX, ALU.max,
                    apply_transpose=True), tB[("s", b, m)][half], last.get(("rmax_read", i)))
            tB[("rmax", b, m)] = t

        def row_max(b, m):
            i = m % 2
            t = PEq([lambda e, k=k: e.transpose(v_ps[0:H, k * P:(k + 1) * P], rmax[i][:, :, k], idn[:]) for k in range(2)],
                    tB[("rmax", b, m)], free["v"])
            last[("rmax_read", i)] = t
            t = V(lambda e: e.tensor_reduce(
                nmax[i][:].rearrange("h (b c) -> h b c", b=2),
                v_ps[0:H, 0:2 * P].rearrange("h (b g c) -> h b c g", b=2, g=4), AXX, ALU.max, negate=True), t,
                last.get(("nmax_read", i)))
            free["v"] = t
            tB[("nmax", b, m)] = t

        def shift_exp(b, m):
            i = m % 2
            t = PEq([lambda e, h=h: e.matmul(s_ps[i][:, h * BS:(h + 1) * BS], hone[:, h, :], nmax[i][:],
                                             start=False, stop=True, skip_group_check=True) for h in range(H)],
                    tB[("nmax", b, m)], *tB[("s", b, m)], tok_hone)
            last[("nmax_read", i)] = t
            t = A(lambda e: e.activation(prob[i][:].rearrange("p h s -> p (h s)"), s_ps[i][:], ACT.Exp, scale=SCALE), t,
                  last.get(("prob_read", i)))
            free["s"][i] = t
            tB[("p", b, m)] = t

        def weighted(b, m):
            i = m % 2
            t = PEq([lambda e, h=h: e.matmul(o_ps[32 * (h % HQ):32 * (h % HQ) + VW, h // HQ, i * BS:(i + 1) * BS],
                                             vaug[i][:, h, :], prob[i][:, h, :], start=True, stop=True)
                     for h in range(H)], tB[("p", b, m)], tB[("v", b, m)], free["o"] if i == 0 else None)
            last[("vaug_read", i)] = last[("prob_read", i)] = t
            tB[("o", b, m)] = t

        def o_rows(b, m):
            t = A(lambda e: e.copy(oT[:].rearrange("p a c -> p (a c)"), o_ps[:].rearrange("p a c -> p (a c)")),
                  tB[("o", b, m)], last.get("oT_read"))
            free["o"] = t
            t = PEq([lambda e, a=a: e.transpose(c_ps[:, a * P:(a + 1) * P], oT[:, a, :], idn[:]) for a in range(HQ)],
                    t, free["c"])
            last["oT_read"] = t
            heads = c_ps[:].rearrange("p (h r) -> p h r", r=VW)
            t = V(lambda e: e.reciprocal(rden[:].rearrange("p (h o) -> p h o", o=1), heads[:, :, HD:HD + 1]), t)
            tB["att"] = V(lambda e: e.tensor_tensor(att[:], heads[:, :, 0:HD],
                                                    rden[:].rearrange("p (h o) -> p h o", o=1).broadcast_to([P, H, HD]), ALU.mult),
                          t, last.get("att_read"))

        def o_columns(b, m):
            t = PEq([lambda e: e.transpose(c_ps[:, 0:P], att[:].rearrange("p h d -> p (h d)"), idn[:])], tB["att"])
            last["att_read"] = t
            tB["attT"] = A(lambda e: e.copy(attT[:], c_ps[:, 0:P]), t, last.get("attT_read"))

        def o_project(b, m):
            k, i = m // 2, b % NX
            t = PEq([lambda e: e.matmul(c_ps[:, P:2 * P], attT[:], wproj[:], start=True, stop=True)], tB["attT"], w_in)
            last["attT_read"] = t
            t = V(lambda e: e.tensor_tensor(x2[i][:, k, :], c_ps[:, P:2 * P], xpb[i][:, k, :], ALU.add), t,
                  tok_xpb[b], tok_store.get(b - NX))
            free["c"] = t
            last[("x2", b)] = t

        sC = {}

        def c_norm(b):
            i = b % NX
            t = norm_stats(x2[i], stats2, mv2, veps2, rstd2, last[("x2", b)])
            sC["stats"] = t

        def c_columns(b):
            i = b % NX
            t = norm_rows(x2[i], mv2, rstd2, xn2, sC["stats"], last.get("xn2_read"))
            last["xn2_read"], sC["xn2T"] = rows_to_columns(xn2, xn2T, t, last.get("xn2T_read"))

        def c_route(b):
            t = PEq([lambda e, k=k: e.matmul(a_ps[:, k * E:(k + 1) * E], xn2T[:, k * P:(k + 1) * P], wrs[:],
                                             start=True, stop=True) for k in range(T)], sC["xn2T"], free["a"], w_in)
            t = V(lambda e: e.tensor_tensor(logit[:], a_ps[:, 0:T * E].rearrange("p (t e) -> p t e", e=E),
                                            brs[:].rearrange("p (o e) -> p o e", o=1).broadcast_to([P, T, E]), ALU.add), t, w_in)
            free["a"] = t
            t1 = V(lambda e: e.tensor_reduce(lmax[:], logit[:], AXX, ALU.max), t)
            t2 = V(lambda e: e.memset(beats[:], 0.0), last.get("beats_read"))
            for d in range(1, E):
                w = E - d
                u = V(lambda e, d=d, w=w: e.tensor_tensor(pair[:, :, 0:w], logit[:, :, 0:w], logit[:, :, d:], ALU.is_ge), t, t2)
                u = V(lambda e, d=d, w=w: e.tensor_tensor(beats[:, :, d:], beats[:, :, d:], pair[:, :, 0:w], ALU.add), u, t2)
                u = V(lambda e, w=w: e.tensor_scalar(nbeats[:, :, 0:w], pair[:, :, 0:w], -1.0, 1.0, ALU.mult, ALU.add), u)
                t2 = V(lambda e, w=w: e.tensor_tensor(beats[:, :, 0:w], beats[:, :, 0:w], nbeats[:, :, 0:w], ALU.add), u)
            t2 = V(lambda e: e.tensor_scalar(beats[:], beats[:], 2.0, None, ALU.is_lt), t2)
            t = V(lambda e: e.tensor_tensor(gexp[:], logit[:], lmax[:].rearrange("p (t o) -> p t o", o=1).broadcast_to([P, T, E]),
                                            ALU.subtract), t1)
            t = A(lambda e: e.activation(gexp[:], gexp[:], ACT.Exp), t)
            t = V(lambda e: e.tensor_tensor(gexp[:], gexp[:], beats[:], ALU.mult), t, t2)
            last["beats_read"] = t
            t = V(lambda e: e.tensor_reduce(gsum[:], gexp[:], AXX, ALU.add), t)
            t = V(lambda e: e.reciprocal(gsum[:], gsum[:]), t)
            sC["gate"] = V(lambda e: e.tensor_tensor(gate[:], gexp[:], gsum[:].rearrange("p (t o) -> p t o", o=1).broadcast_to([P, T, E]),
                                                     ALU.mult), t)

        def c_gate_rows(b):
            i = b % NX
            t = PEq([lambda e, k=k: e.transpose(a_ps[0:E, k * P:(k + 1) * P], gate[:, k, :], idn[:]) for k in range(T)],
                    sC["gate"], free["a"])
            t = A(lambda e: e.copy(gateT[:], a_ps[0:E, :]), t, last.get("gateT_read"))
            t = PEq([lambda e, k=k: e.matmul(a_ps[:, k * P:(k + 1) * P], gateT[:, k * P:(k + 1) * P], mexp[:],
                                             start=True, stop=True) for k in range(T)], t, tok_mexp)
            last["gateT_read"] = t
            t = V(lambda e: e.tensor_tensor(x2[i][:].rearrange("p t d -> p (t d)"), x2[i][:].rearrange("p t d -> p (t d)"),
                                            a_ps[:], ALU.add), t)
            free["a"] = t
            sC["acc"] = [t] * T

        up_ps = [s_ps[0][:, 0:N], s_ps[0][:, N:], s_ps[1][:, 0:N], s_ps[1][:, N:]]

        def c_up(b, x):
            for c in range(C):
                t = PEq([lambda e, c=c: e.matmul(up_ps[c], w1s[:, x, c * P:(c + 1) * P], xn2T[:], start=True, stop=True)],
                        sC["xn2T"], free["s"][0], free["s"][1], sC.get(("up", c)), w_in)
                last["xn2T_read"] = t
                sC[("up", c)] = A(lambda e, c=c: e.activation(hid[x % 2][:, c, :], up_ps[c], ACT.Gelu,
                                                              bias=b1s[:, x * C + c:x * C + c + 1]), t, last.get(("hid", x % 2)))
                sC[("h", x, c)] = sC[("up", c)]

        def c_down(b, x):
            i = b % NX
            key, y_ps = ("o", o_ps[:].rearrange("p a c -> p (a c)")) if x % 2 == 0 else ("c", c_ps[:])
            for k in range(T):
                t = PEq([lambda e, c=c, k=k: e.matmul(y_ps[:, k * P:(k + 1) * P], hid[x % 2][:, c, k * P:(k + 1) * P],
                                                      w2s[:, x * C + c, :], start=(c == 0), stop=(c == C - 1))
                         for c in range(C)], *[sC[("h", x, c)] for c in range(C)], free[key] if k == 0 else None)
            last[("hid", x % 2)] = t
            for k in range(T):
                sC["acc"][k] = V(lambda e, k=k: e.scalar_tensor_tensor(
                    x2[i][:, k, :], y_ps[:, k * P:(k + 1) * P], gate[:, k, x:x + 1], x2[i][:, k, :], ALU.mult, ALU.add),
                    t, sC["acc"][k])
            free[key] = sC["acc"][T - 1]

        def experts(b, store, stored):
            c_up(b, 0)
            for x in range(1, E):
                c_up(b, x)
                c_down(b, x - 1)
            c_down(b, E - 1)
            tok_store[b] = run.put("sync", store, sC["acc"], stored)
            t = sC[("up", C - 1)]
            free["s"] = [t, t]

        def store_of(b):
            return lambda e: e.dma_start(out[b].rearrange("(t p) d -> p t d", p=P), x2[b % NX][:]), out_done[b % NX]

        def general_select():
            for part, dst, total in ((0, gq, qsum), (1, gk, ksum)):
                t = project(part, 0)
                A(lambda e, dst=dst: e.copy(dst[:], a_ps[:]), t)
                sA["g"] = (run.act.sem, run.act.count)
                free["a"] = V(lambda e, total=total: e.tensor_reduce(
                    total[:], a_ps[:].rearrange("p (m s) -> p m s", s=BS), AXX, ALU.add), sA["g"])
            sA["qk"] = V(lambda e: e.tensor_tensor(
                qk[:], qsum[:].rearrange("p (m o) -> p m o", o=1).broadcast_to([P, M, M]),
                ksum[:].rearrange("p (o n) -> p o n", o=1).broadcast_to([P, M, M]), ALU.mult), free["a"])
            t = PEq([lambda e, k=k: e.matmul(c_ps[:, k * P:(k + 1) * P], xnT[:, k * P:(k + 1) * P], wqkv[:, 2 * D:],
                                             start=True, stop=True) for k in range(T)], sA["xnT"])
            sA["gv"] = free["c"] = A(lambda e: e.copy(gv[:].rearrange("p t d -> p (t d)"), c_ps[:]), t)
            t = products()
            t = V(lambda e: e.tensor_tensor(ceq[:], ceq[:], own[:], ALU.max), t)
            t = V(lambda e: e.tensor_scalar(ceq[:], ceq[:], -1.0, FAR, ALU.add, ALU.mult), t)
            t = PEq([lambda e: e.transpose(a_ps[0:M * M, 0:P], ceq[:].rearrange("p m n -> p (m n)"), idn[:])], t, free["a"])
            sA["bias"] = free["a"] = V(lambda e: e.tensor_copy(gbias[:], a_ps[0:M * M, 0:P]), t)

        def general_heads():
            read, filled, done = None, None, {}
            for h in range(H):
                tq = V(lambda e, h=h: e.tensor_scalar(gqh[:], gq[:], hmask[:, h:h + 1], None, ALU.mult), sA["g"], read)
                tb = V(lambda e, h=h: e.tensor_scalar(gbh[:], qrows[:], gbias[:, h * HD:h * HD + 1], None, ALU.mult),
                       sA["bias"], read)
                for k in range(T):
                    s = s_ps[0][:, 0:N]
                    read = PEq([lambda e, k=k: e.matmul(s, gqh[:, k * P:(k + 1) * P], gk[:], start=True, stop=False),
                                lambda e, k=k: e.matmul(s, gbh[:, k * P:(k + 1) * P], krows[:], start=False, stop=True)],
                               tq, tb, done.get("exp"))
                    t = V(lambda e: e.tensor_reduce(gmax[:], s, AXX, ALU.max, negate=True), read, done.get("exp"))
                    t = V(lambda e: e.tensor_scalar(gmax[:], gmax[:], SCALE, None, ALU.mult), t)
                    done["exp"] = A(lambda e: e.activation(gp[:], s, ACT.Exp, bias=gmax[:], scale=SCALE, accum_out=gsumr[:]),
                                    t, done.get("tr"), done.get("norm"))
                    done["tr"] = PEq([lambda e, c=c: e.transpose(s_ps[1][:, c * P:(c + 1) * P], gp[:, c * P:(c + 1) * P], idn[:])
                                      for c in range(T)], done["exp"], filled)
                    filled = A(lambda e: e.copy(gpT[:], s_ps[1][:, 0:N]), done["tr"], done.get("pv"))
                    done["pv"] = PEq([lambda e, c=c, h=h: e.matmul(v_ps[:, 0:HD], gpT[:, c * P:(c + 1) * P],
                                                                   gv[:, c, h * HD:(h + 1) * HD], start=(c == 0), stop=(c == T - 1))
                                      for c in range(T)], filled, sA["gv"], done.get("norm"))
                    t = V(lambda e: e.reciprocal(gsumr[:], gsumr[:]), done["exp"])
                    done["norm"] = V(lambda e, k=k, h=h: e.tensor_scalar(gatt[:, k, h * HD:(h + 1) * HD], v_ps[:, 0:HD], gsumr[:],
                                                                         None, ALU.mult), t, done["pv"])
            for k in range(T):
                t = PEq([lambda e, k=k: e.transpose(c_ps[:, 0:P], gatt[:, k, :], idn[:])], done["norm"], free["c"])
                tB["attT"] = A(lambda e: e.copy(attT[:], c_ps[:, 0:P]), t, last.get("attT_read"))
                o_project(0, 2 * k)

        a_norm(0)
        a_q(0)
        a_k(0)
        a_v(0)
        a_select(0)
        for b in range(B):
            fill = {}
            if b + 2 < B:
                fill.setdefault(0, []).append(lambda: load_x(b + 2))
            if b + 1 < B:
                fill.setdefault(0, []).append(lambda: a_norm(b + 1))
                fill.setdefault(1, []).append(lambda: a_q(b + 1))
                fill.setdefault(2, []).append(lambda: a_k(b + 1))
                fill.setdefault(3, []).append(lambda: a_v(b + 1))
                fill.setdefault(4, []).append(lambda: a_select(b + 1))
            if b >= 1:
                fill.setdefault(4, []).append(lambda: c_norm(b - 1))
                fill.setdefault(5, []).append(lambda: c_columns(b - 1))
                fill.setdefault(6, []).append(lambda: c_route(b - 1))
                fill.setdefault(7, []).append(lambda: c_gate_rows(b - 1))
            scores(b, 0)
            values(b, 0)
            block_max(b, 0)
            for m in range(M):
                row_max(b, m)
                if m >= 1:
                    weighted(b, m - 1)
                shift_exp(b, m)
                if m + 1 < M:
                    scores(b, m + 1)
                    block_max(b, m + 1)
                if m % 2 == 0 and m >= 2:
                    o_rows(b, m - 1)
                if m + 1 < M:
                    values(b, m + 1)
                for f in fill.get(m, []):
                    f()
                if m % 2 == 0 and m >= 2:
                    o_columns(b, m - 1)
                    o_project(b, m - 1)
            weighted(b, M - 1)
            o_rows(b, M - 1)
            o_columns(b, M - 1)
            o_project(b, M - 1)
            if b >= 1:
                experts(b - 1, *store_of(b - 1))
        c_norm(B - 1)
        c_columns(B - 1)
        c_route(B - 1)
        c_gate_rows(B - 1)
        experts(B - 1, *store_of(B - 1))
        for b in range(B - NX, B):
            run.put("sync", lambda e: e.nop(), [tok_store[b]])

        t = V(lambda e: e.tensor_reduce(tiemax[:], ties[:].rearrange("p b m -> p (b m)"), AXX, ALU.max), last["ties"])
        t = PEq([lambda e: e.transpose(a_ps[0:1, 0:P], tiemax[:], idn[:])], t, free["a"])
        t = V(lambda e: e.tensor_reduce(tieall[:], a_ps[0:1, 0:P], AXX, ALU.max), t)
        V(lambda e: e.tensor_scalar(tieflag[:], tieall[:], 1.5, None, ALU.is_gt), t)
        run.block(nc)

        tied = nc.values_load(tieflag[0:1, 0:1], min_val=0, max_val=1)
        with nc.If(tied > 0):
            with nc.Fori(0, B) as batch:
                run = Run(ev, "general")
                g_x, g_out = ev("g_x", 16), ev("g_out", 16)
                free = {"a": None, "v": None, "c": None, "o": None, "s": [None, None]}
                for d in (last, sA, tB, sC, tok_xpb, tok_xn, tok_store):
                    d.clear()
                tok_x[0] = run.put("sync", lambda e: e.dma_start(
                    xs[0][:], x[bass.ds(batch, 1)].rearrange("o (t p) d -> p (o t) d", p=P)), (), g_x)
                a_norm(0)
                general_select()
                general_heads()
                c_norm(0)
                c_columns(0)
                c_route(0)
                c_gate_rows(0)
                experts(0, lambda e: e.dma_start(
                    out[bass.ds(batch, 1)].rearrange("o (t p) d -> p (o t) d", p=P), x2[0][:]), g_out)
                run.put("sync", lambda e: e.nop(), [tok_store[0]])
                run.block(nc)
                nc.all_engine_barrier(sems_to_clear=range(run.dve.sem.num, g_out.sem.num + 1))


def constants():
    p = np.arange(P)
    f = np.float32
    head_one = np.zeros((H, H, P), f)
    head_one[np.arange(H), np.arange(H)] = 1
    expert_rows = np.zeros((P, E, C, E), f)
    expert_rows[:, np.arange(E), :, np.arange(E)] = 1
    return {
        "ident": np.eye(P, dtype=f),
        "quad_mask": (p[:, None] // HD % HQ == np.arange(HQ)).astype(f),
        "head_sum": (p[:, None] // HD == p // HD).astype(f),
        "head_one": head_one,
        "block_rank": np.broadcast_to((M - np.arange(M)).astype(f), (P, M, M)).copy(),
        "row_base": (p[:, None] * M + M).astype(f),
        "expert_rows": expert_rows,
        "own_block": np.broadcast_to(np.eye(M, dtype=f), (P, M, M)).copy(),
        "head_mask": (p[:, None] // HD == np.arange(H)).astype(f),
        "query_rows": (np.arange(M * M)[:, None] // M == np.arange(N) // BS).astype(f),
        "key_rows": (np.arange(M * M)[:, None] % M == np.arange(N) // BS).astype(f),
    }


def kernel(**inputs):
    import concourse.bacc as bacc
    from concourse.bass_utils import run_bass_kernel_spmd

    a = {k: np.ascontiguousarray(v) for k, v in inputs.items()}
    arrays = {
        "x": a["L0_attn_x"],
        "wqkv_t": np.ascontiguousarray(a["L0_attn_qkv_w"].T),
        "wproj_t": np.ascontiguousarray(a["L0_attn_proj_w"].T),
        "proj_b": np.ascontiguousarray(np.broadcast_to(a["L0_attn_proj_b"], (P, D))),
        "w1": a["L0_ffn_w1"],
        "b1_t": np.ascontiguousarray(a["L0_ffn_b1"].reshape(E * C, P).T),
        "w2": a["L0_ffn_w2"],
        "b2": a["L0_ffn_b2"],
        "wr": a["L0_ffn_wr"],
        "br": np.ascontiguousarray(np.broadcast_to(a["L0_ffn_br"], (P, E))),
    } | constants()
    nc = bacc.Bacc("TRN2", target_bir_lowering=False, num_devices=1)
    args = {k: nc.dram_tensor(f"in_{k}", v.shape, mybir.dt.from_np(v.dtype), kind="ExternalInput").ap()
            for k, v in arrays.items()}
    out = nc.dram_tensor("out_x", (B, N, D), F32, kind="ExternalOutput").ap()
    layer(nc, **args, out=out)
    r = run_bass_kernel_spmd(nc, [{f"in_{k}": v for k, v in arrays.items()}], core_ids=[0])
    return r.results[0]["out_x"]
```

```python
from contextlib import ExitStack

import numpy as np

import concourse.bass as bass
from concourse import mybir

F32 = mybir.dt.float32
F32R = mybir.dt.float32r
BF16 = mybir.dt.bfloat16
U32 = mybir.dt.uint32
ALU = mybir.AluOpType
ACT = mybir.ActivationFunctionType
AXX = mybir.AxisListType.X

P = 128
B, N, D = 16, 512, 128
H = 16
HD = D // H
BS = 64
M = N // BS
T = N // P
SCALE = HD ** -0.5
EPS = 1e-5
E, HID = 4, 512
C = HID // P
QUADS = 4
HQ = H // QUADS
KEYS = 2 * BS
ROW = 3 * BS
FAR = 1e30
VW = 32


class Event:

    def __init__(self, sem, step=1):
        self.sem, self.step, self.count = sem, step, 0

    def tick(self):
        self.count += self.step
        return self.sem, self.count


class Run:

    def __init__(self, event, name):
        self.dve, self.pool, self.act, self.pe = (event(f"{name}_{e}") for e in ("dve", "pool", "act", "pe"))
        self.lists = {e: [] for e in ("sync", "gpsimd", "scalar", "vector", "tensor")}
        self.waited = {e: {} for e in self.lists}

    def put(self, engine, emit, after=(), done=None):
        waits = []
        for token in after:
            if token is None:
                continue
            sem, value = token
            if self.waited[engine].get(id(sem), 0) < value:
                self.waited[engine][id(sem)] = value
                waits.append(token)
        token = done.tick() if done else None
        self.lists[engine].append((waits, emit, done))
        return token

    def block(self, nc):
        with nc.Block() as block:
            block.sync(lambda eng: self.play("sync", eng))
            block.gpsimd(lambda eng: self.play("gpsimd", eng))
            block.scalar(lambda eng: self.play("scalar", eng))
            block.vector(lambda eng: self.play("vector", eng))
            block.tensor(lambda eng: self.play("tensor", eng))

    def play(self, engine, eng):
        for waits, emit, done in self.lists[engine]:
            for sem, value in waits:
                eng.wait_ge(sem, value)
            ins = emit(eng)
            if done:
                ins.then_inc(done.sem, done.step)


def layer(nc, x, wqkv_t, wproj_t, proj_b, w1, b1_t, w2, b2, wr, br, ident, quad_mask, head_sum,
          head_one, block_rank, row_base, expert_before, expert_rows, own_block, head_mask,
          query_rows, key_rows, out):
    with ExitStack() as ctx:
        def sb(name, shape, dt=F32):
            return ctx.enter_context(nc.sbuf_tensor(name, shape, dt))

        def ps(name, shape, dt=F32):
            return ctx.enter_context(nc.psum_tensor(name, shape, dt))

        def ev(name, step=1):
            return Event(ctx.enter_context(nc.semaphore(name)), step)

        wqkv = sb("wqkv", [P, 3 * D])
        wproj = sb("wproj", [P, D])
        projb = sb("projb", [P, D])
        w1hi, w1lo = sb("w1hi", [P, E, HID], F32R), sb("w1lo", [P, E, HID], F32R)
        w2s = sb("w2s", [P, E * C, D])
        b1s = sb("b1s", [P, E * C])
        b2s = sb("b2s", [E, D])
        wrs = sb("wrs", [P, E])
        brs = sb("brs", [P, E])
        idn = sb("idn", [P, P])
        qmask = sb("qmask", [P, HQ])
        hsum = sb("hsum", [P, P])
        hone32 = sb("hone32", [H, H, P])
        hone = sb("hone", [H, H, P], BF16)
        rank = sb("rank", [P, M, M])
        rbase = sb("rbase", [P, 1])
        erows = sb("erows", [P, E, C, E])
        neg_half = sb("neg_half", [P, T])
        ones4 = sb("ones4", [E, E])
        g1 = sb("g1", [P, E, C])
        g1m = sb("g1m", [P, E, C, E])
        cexp = sb("cexp", [E, D])
        mexp = sb("mexp", [E, D])

        NX, N2 = 2, 4
        xs = [sb(f"xs{i}", [P, T, D]) for i in range(NX)]
        xpb = [sb(f"xpb{i}", [P, T, D]) for i in range(NX)]
        x2 = [sb(f"x2{i}", [P, T, D]) for i in range(N2)]
        stats = sb("stats", [P, T, 6])
        mv = sb("mv", [P, T, 2])
        veps = sb("veps", [P, T])
        rstd = sb("rstd", [P, T])
        xn = sb("xn", [P, T, D])
        xnT = sb("xnT", [P, N])
        qhi = sb("qhi", [P, N], F32R)
        qlo = sb("qlo", [P, N])
        qmh = [sb(f"qmh{i}", [P, HQ, N], F32R) for i in range(2)]
        qml = [sb(f"qml{i}", [P, HQ, N], F32R) for i in range(2)]
        stage = [sb(f"stage{i}", [P, M, BS, 3], F32R) for i in range(2)]
        kv = [sb(f"kv{i}", [P, M, KEYS, 3], F32R) for i in range(2)]
        qsum = sb("qsum", [P, M])
        ksum = sb("ksum", [P, M])
        qk = sb("qk", [P, M, M])
        crow = sb("crow", [P, M, M])
        cmax = sb("cmax", [P, M])
        ceq = sb("ceq", [P, M, M])
        crank = sb("crank", [P, M, M])
        cbest = sb("cbest", [P, M])
        index = [sb(f"index{i}", [P, M], U32) for i in range(2)]
        ties = sb("ties", [P, B, M])
        vaug = [sb(f"vaug{i}", [P, H, VW]) for i in range(2)]
        rmax = [sb(f"rmax{i}", [P, H, 2], BF16) for i in range(2)]
        idn16 = sb("idn16", [P, P], BF16)
        nmax = [sb(f"nmax{i}", [H, BS], BF16) for i in range(2)]
        prob = [sb(f"prob{i}", [P, H, BS]) for i in range(2)]
        oT = sb("oT", [P, HQ, P])
        rden = sb("rden", [P, H])
        att = sb("att", [P, H, HD])
        attT = sb("attT", [P, P])
        stats2 = sb("stats2", [P, T, 6])
        mv2 = sb("mv2", [P, T, 2])
        veps2 = sb("veps2", [P, T])
        rstd2 = sb("rstd2", [P, T])
        xn2 = sb("xn2", [P, T, D])
        tiemax, tieall = sb("tiemax", [P, 1]), sb("tieall", [1, 1])
        tieflag = sb("tieflag", [1, 1], U32)
        own = sb("own", [P, M, M])
        hmask = sb("hmask", [P, H])
        qrows = sb("qrows", [M * M, N])
        krows = sb("krows", [M * M, N])
        gbias = sb("gbias", [M * M, P])
        gmax, gsumr = sb("gmax", [P, 1]), sb("gsumr", [P, 1])
        xn2T = sb("xn2T", [P, N])
        xn2hi, xn2lo = sb("xn2hi", [P, N], F32R), sb("xn2lo", [P, N], F32R)
        logit = sb("logit", [P, T, E])
        beats = sb("beats", [P, T, E])
        level, before = sb("level", [P, T, E, E]), sb("before", [P, T, E, E])
        earlier = sb("earlier", [P, T, E, E])
        lmax = sb("lmax", [P, T])
        gexp = sb("gexp", [P, T, E])
        gsum = sb("gsum", [P, T])
        gate = [sb(f"gate{i}", [P, T, E]) for i in range(2)]
        gateT = sb("gateT", [E, N])
        hid = sb("hid", [P, E * C, N])
        w1_landing = hid[:, 0:E, :]
        gq, gk, gqh, gbh, gp, gpT, gv, gatt = (hid[:, n, :] for n in range(8))
        gv, gatt = (r.rearrange("p (t d) -> p t d", d=D) for r in (gv, gatt))
        gbh = gbh[0:M * M, :]

        table = [nc.dram_tensor(f"kv_table{b}", [P * M, ROW], F32, kind="Internal").ap() for b in range(B)]

        s_ps = [ps(f"s_ps{i}", [P, 2 * N]) for i in range(2)]
        o_ps = ps("o_ps", [P, HQ, P])
        v_ps = ps("v_ps", [P, N])
        a_ps = ps("a_ps", [P, N])
        y_ps = ps("y_ps", [P, N])

        weights_in, attention_in, experts_in = (ev(name, 16) for name in ("weights_in", "attention_in", "experts_in"))
        x_in = [ev(f"x_in{i}", 16) for i in range(NX)]
        table_out = [ev(f"table_out{i}", 16) for i in range(2)]
        own_in = [ev(f"own_in{i}", 16) for i in range(2)]
        sel_in = [[ev(f"sel_in{i}_{m}", 16) for m in range(M)] for i in range(2)]
        out_done = [ev(f"out_done{i}", 16) for i in range(N2)]
        run = Run(ev, "fast")

        def V(emit, *after):
            return run.put("vector", emit, after, run.dve)

        def G(emit, *after):
            return run.put("gpsimd", emit, after, run.pool)

        def A(emit, *after):
            return run.put("scalar", emit, after, run.act)

        def PEq(emits, *after):
            for n, emit in enumerate(emits):
                token = run.put("tensor", emit, after if n == 0 else (), run.pe if n == len(emits) - 1 else None)
            return token

        first = [(idn, ident), (wqkv, wqkv_t), (projb, proj_b), (qmask, quad_mask)]
        second = [(hsum, head_sum), (rank, block_rank), (rbase, row_base), (hone32, head_one), (wproj, wproj_t)]
        third = [(b1s, b1_t), (w2s, w2.rearrange("e (c p) d -> p (e c) d", p=P)), (b2s, b2), (earlier, expert_before), (erows, expert_rows),
                 (w1_landing, w1.rearrange("e d h -> d e h")), (wrs, wr), (brs, br), (own, own_block),
                 (hmask, head_mask), (qrows, query_rows), (krows, key_rows)]
        tok_x, tok_xpb, tok_xn, tok_store = {}, {}, {}, {}

        def load_x(b):
            i = b % NX
            tok_x[b] = run.put("sync", lambda e: e.dma_start(
                xs[i][:], x[b].rearrange("(t p) d -> p t d", p=P)),
                [tok_xpb.get(b - NX), tok_xn.get(b - NX)], x_in[i])

        def load(arrays, arrived):
            for dst, src in arrays:
                token = run.put("sync", lambda e, dst=dst, src=src: e.dma_start(dst if isinstance(dst, bass.AP) else dst[:], src), (), arrived)
            return token

        load_x(0)
        w_in = load(first, weights_in)
        w_att = load(second, attention_in)
        w_exp = load(third, experts_in)
        load_x(1)

        c0 = V(lambda e: e.memset(neg_half[:], -0.5))
        c_ones = V(lambda e: e.memset(ones4[:], 1.0))
        for i in range(2):
            t = V(lambda e, i=i: e.memset(vaug[i][:], 0.0))
        for i in range(2):
            c1 = V(lambda e, i=i: e.memset(vaug[i][:, :, HD:HD + 1], 1.0), t)

        free = {"a": None, "v": None, "y": None, "o": None, "s": [None, None]}
        last = {}
        sE = {}

        def hidden_of_bias():
            t = A(lambda e: e.activation(g1[:], b1s[:].rearrange("p (e c) -> p e c", e=E), ACT.Gelu), w_exp)
            sE["g1m"] = V(lambda e: e.tensor_tensor(g1m[:], erows[:], g1[:].rearrange("p e (c o) -> p e c o", o=1).broadcast_to([P, E, C, E]),
                                                    ALU.mult), t, w_exp)

        def split_w1(x):
            t = G(lambda e: e.tensor_copy(w1hi[:, x, :], w1_landing[:, x, :]), w_exp)
            sE["w1"] = last[("hid_read", 0)] = G(lambda e: e.tensor_tensor(
                w1lo[:, x, :], w1_landing[:, x, :], w1hi[:, x, :].bitcast(F32), ALU.subtract), t)

        def expert_rows_sum():
            t = PEq([lambda e, k=k: e.matmul(a_ps[0:E, 0:D], g1m[:, k // C, k % C, :], w2s[:, k, :],
                                             start=(k == 0), stop=(k == E * C - 1)) for k in range(E * C)], sE["g1m"], free["a"])
            t = V(lambda e: e.tensor_tensor(cexp[:], a_ps[0:E, 0:D], b2s[:], ALU.add), t)
            t = PEq([lambda e: e.matmul(a_ps[0:E, 0:D], ones4[:], cexp[:], start=True, stop=True)], t, c_ones)
            t = free["a"] = V(lambda e: e.tensor_tensor(mexp[:], a_ps[0:E, 0:D], cexp[:], ALU.subtract), t)
            sE["m"] = V(lambda e: e.tensor_tensor(mexp[:], mexp[:], b2s[:], ALU.add), t)

        def norm_stats(src, st, m_v, ve, rs, tok_src):
            for k in range(T):
                t = V(lambda e, k=k: e.bn_stats(st[:, k, :], src[:, k, :]), tok_src)
            for k in range(T):
                t2 = V(lambda e, k=k: e.bn_aggr(m_v[:, k, :], st[:, k, :]), t)
            t = G(lambda e: e.tensor_scalar(ve[:], m_v[:, :, 1], EPS, None, ALU.add), t2)
            return G(lambda e: e.tensor_tensor(rs[:], ve[:], neg_half[:], ALU.pow), t, c0)

        def norm_rows(src, m_v, rs, dst, tok, free_dst):
            for k in range(T):
                t = V(lambda e, k=k: e.tensor_scalar(dst[:, k, :], src[:, k, :], m_v[:, k, 0:1],
                                                     rs[:, k:k + 1], ALU.subtract, ALU.mult), tok, free_dst)
            return t

        def rows_to_columns(src, dst, tok, *free_dst):
            t = PEq([lambda e, k=k: e.transpose(a_ps[:, k * P:(k + 1) * P], src[:, k, :], idn[:])
                     for k in range(T)], tok, free["a"], w_in)
            free["a"] = A(lambda e: e.copy(dst[:], a_ps[:]), t, *free_dst)
            return t, free["a"]

        sA = {}

        def a_stats(b):
            sA["rstd"] = norm_stats(xs[b % NX], stats, mv, veps, rstd, tok_x[b])

        def a_rows(b):
            i = b % NX
            tok_xpb[b] = G(lambda e: e.tensor_tensor(
                xpb[i][:], xs[i][:], projb[:].rearrange("p (o d) -> p o d", o=1).broadcast_to([P, T, D]), ALU.add),
                tok_x[b], w_in, last.get(("x2", b - NX)))
            sA["xn"] = tok_xn[b] = norm_rows(xs[i], mv, rstd, xn, sA["rstd"], last.get("xn_read"))

        def a_columns(b):
            last["xn_read"], sA["xnT"] = rows_to_columns(xn, xnT, sA["xn"], last.get("xnT_read"))

        def project(part, b):
            t = PEq([lambda e: e.matmul(a_ps[:], wqkv[:, part * D:(part + 1) * D], xnT[:],
                                        start=True, stop=True)], sA["xnT"], free["a"], w_in)
            last["xnT_read"] = t
            return t

        def a_project_q(b):
            sA["q_ps"] = project(0, b)

        def a_q(b):
            t = sA["q_ps"]
            sA["qhi"] = V(lambda e: e.tensor_copy(qhi[:], a_ps[:]), t, last.get("qhi_read"))
            V(lambda e: e.tensor_reduce(qsum[:], a_ps[:].rearrange("p (m s) -> p m s", s=BS), AXX, ALU.add), t)
            sA["qlo"] = free["a"] = V(lambda e: e.tensor_tensor(qlo[:], a_ps[:], qhi[:].bitcast(F32), ALU.subtract),
                                      sA["qhi"], last.get("qlo_read"))

        def a_mask_q(b, heads):
            j = b % 2
            for h in heads:
                last["qhi_read"] = V(lambda e, h=h: e.tensor_scalar(qmh[j][:, h, :], qhi[:].bitcast(F32), qmask[:, h:h + 1],
                                                                    None, ALU.mult), sA["qhi"], w_in, last.get(("q_read", j)))
                last["qlo_read"] = G(lambda e, h=h: e.tensor_scalar(qml[j][:, h, :], qlo[:], qmask[:, h:h + 1],
                                                                    1.0, ALU.mult, ALU.mult), sA["qlo"], w_in, last.get(("q_read", j)))
            sA[("q", b)] = (last["qhi_read"], last["qlo_read"])

        def a_project_k(b):
            sA["k_ps"] = project(1, b)

        def a_k(b):
            j = b % 2
            st = stage[j]
            kview = a_ps[:].rearrange("p (m s) -> p m s", s=BS)
            hi = V(lambda e: e.tensor_copy(st[:, :, :, 0], kview), sA["k_ps"], last.get(("stage_read", j)), last.get(("stage_read2", j)))
            V(lambda e: e.tensor_reduce(ksum[:], kview, AXX, ALU.add), sA["k_ps"])
            free["a"] = V(lambda e: e.tensor_tensor(st[:, :, :, 1], kview, st[:, :, :, 0].bitcast(F32),
                                                    ALU.subtract), hi)
            sA["k"] = free["a"]

        def a_qk(b):
            sA["qk"] = V(lambda e: e.tensor_tensor(
                qk[:], qsum[:].rearrange("p (m o) -> p m o", o=1).broadcast_to([P, M, M]),
                ksum[:].rearrange("p (o n) -> p o n", o=1).broadcast_to([P, M, M]), ALU.mult), sA["k"])

        def a_v(b):
            j = b % 2
            st = stage[j]
            t = project(2, b)
            free["a"] = A(lambda e: e.copy(st[:, :, :, 2].bitcast(F32), a_ps[:].rearrange("p (m s) -> p m s", s=BS)),
                          t, last.get(("stage_read", j)), last.get(("stage_read2", j)))
            tb = run.put("sync", lambda e: e.dma_start(
                table[b][:, :].rearrange("(p n) c -> p (n c)", n=M), st[:].bitcast(F32).rearrange("p n s c -> p (n s c)")),
                [free["a"], sA["k"]], table_out[j])
            own_t = run.put("sync", lambda e: e.dma_start(
                kv[j][:, :, 0:BS, :].bitcast(F32).rearrange("p m s c -> p m (s c)"), st[:].bitcast(F32).rearrange("p m s c -> p m (s c)")),
                [last.get(("kv_read", j))], own_in[j])
            last[("stage_read", j)], last[("stage_read2", j)] = tb, own_t
            sA[("own", b)] = own_t
            sA["table"] = tb

        def a_products(b):
            sA["c_ps"] = PEq([lambda e: e.matmul(a_ps[:, 0:M * M], hsum[:], qk[:].rearrange("p m n -> p (m n)"),
                                        start=True, stop=True)], sA["qk"], free["a"], w_att)

        def best_blocks():
            t = V(lambda e: e.tensor_scalar(crow[:].rearrange("p m n -> p (m n)"), a_ps[:, 0:M * M],
                                            1.0 / (BS * BS), SCALE, ALU.mult, ALU.mult), sA["c_ps"])
            free["a"] = t
            t = V(lambda e: e.tensor_reduce(cmax[:], crow[:], AXX, ALU.max), t)
            return V(lambda e: e.tensor_tensor(ceq[:], crow[:], cmax[:].rearrange("p (m o) -> p m o", o=1).broadcast_to([P, M, M]),
                                               ALU.is_ge), t)

        def a_select(b):
            j = b % 2
            t = best_blocks()
            last["ties"] = V(lambda e: e.tensor_reduce(ties[:, b, :], ceq[:], AXX, ALU.add), t)
            t = V(lambda e: e.tensor_tensor(crank[:], ceq[:], rank[:], ALU.mult), t, w_att)
            t = V(lambda e: e.tensor_reduce(cbest[:], crank[:], AXX, ALU.max), t)
            t = V(lambda e: e.tensor_scalar(index[j][:], cbest[:], -1.0, rbase[:], ALU.mult, ALU.add), t,
                  *(sA.get(("sel", b - 2, m)) for m in range(M)))
            for m in range(M):
                g = run.put("gpsimd", lambda e, m=m: e.indirect_dma_start(
                    out=kv[j][:, m, BS:, :].bitcast(F32).rearrange("p s c -> p (s c)"), out_offset=None, in_=table[b][:, :],
                    in_offset=bass.IndirectOffsetOnAxis(ap=index[j][:, m:m + 1], axis=0)),
                    [t, sA["table"], last.get(("kv_read", j))], sel_in[j][m])
                sA[("sel", b, m)] = g

        tB = {}

        def scores(b, m):
            j, i = b % 2, m % 2
            keys_hi = kv[j][:, m, :, 0]
            keys_lo = kv[j][:, m, :, 1]
            halves = []
            for g, bank_first in ((0, True), (2, True), (1, False), (3, False)):
                r = slice(32 * g, 32 * g + 32)
                dst = s_ps[i][:, g * HQ * BS:(g + 1) * HQ * BS].rearrange("p (h s) -> p h s", s=BS)
                qh = qmh[j][r, :, m * BS:(m + 1) * BS]
                ql = qml[j][r, :, m * BS:(m + 1) * BS]
                emits = [lambda e, l=l, rr=rr, s=s, dst=dst: e.matmul(dst, l, rr, start=s, stop=False, skip_group_check=True)
                         for l, rr, s in ((keys_hi[r], qh, bank_first), (keys_hi[r], ql, False), (keys_lo[r], qh, False))]
                halves.append(PEq(emits, halves[-2] if len(halves) >= 2 else None, *sA[("q", b)], sA[("own", b)], sA[("sel", b, m)], free["s"][i]))
            tB[("s", b, m)] = halves[2], halves[3]
            last[("q_read", j)] = halves[3]

        def values(b, m):
            j, i = b % 2, m % 2
            t = PEq([lambda e: e.transpose(v_ps[:, 0:P], kv[j][:, m, :, 2].bitcast(F32), idn[:])],
                    sA[("own", b)], sA[("sel", b, m)], free["v"])
            last[("kv_read", j)] = t
            t = A(lambda e: e.copy(vaug[i][:, :, 0:HD], v_ps[:, 0:P].rearrange("p (h d) -> p h d", d=HD)), t, c1,
                  last.get(("vaug_read", i)))
            free["v"] = t
            tB[("v", b, m)] = t

        def block_max(b, m):
            i = m % 2
            for half in range(2):
                t = V(lambda e, half=half: e.tensor_reduce(
                    rmax[i][:, half * 8:(half + 1) * 8, :],
                    s_ps[i][:, half * N:(half + 1) * N].rearrange("p (a c) -> p a c", c=32), AXX, ALU.max,
                    apply_transpose=True), tB[("s", b, m)][half], last.get(("rmax_read", i)))
            tB[("rmax", b, m)] = t

        def row_max(b, m):
            i = m % 2
            t = PEq([lambda e, k=k: e.transpose(v_ps[0:H, k * P // 2:(k + 1) * P // 2].bitcast(BF16), rmax[i][:, :, k], idn16[:]) for k in range(2)],
                    tB[("rmax", b, m)], free["v"], tok_idn16)
            last[("rmax_read", i)] = t
            t = V(lambda e: e.tensor_reduce(
                nmax[i][:].rearrange("h (b c) -> h b c", b=2),
                v_ps[0:H, 0:P].bitcast(BF16).rearrange("h (b g c) -> h b c g", b=2, g=4), AXX, ALU.max, negate=True), t,
                last.get(("nmax_read", i)))
            free["v"] = t
            tB[("nmax", b, m)] = t

        def shift_exp(b, m):
            i = m % 2
            t = PEq([lambda e, h=h: e.matmul(s_ps[i][:, h * BS:(h + 1) * BS], hone[:, h, :], nmax[i][:],
                                             start=False, stop=True, skip_group_check=True) for h in range(H)],
                    tB[("nmax", b, m)], *tB[("s", b, m)], tok_hone)
            last[("nmax_read", i)] = t
            t = A(lambda e: e.activation(prob[i][:].rearrange("p h s -> p (h s)"), s_ps[i][:], ACT.Exp, scale=SCALE), t,
                  last.get(("prob_read", i)))
            free["s"][i] = t
            tB[("p", b, m)] = t

        def weighted(b, m):
            i = m % 2
            t = PEq([lambda e, h=h: e.matmul(o_ps[32 * (h % HQ):32 * (h % HQ) + VW, h // HQ, i * BS:(i + 1) * BS],
                                             vaug[i][:, h, :], prob[i][:, h, :], start=True, stop=True)
                     for h in range(H)], tB[("p", b, m)], tB[("v", b, m)], free["o"] if i == 0 else None)
            last[("vaug_read", i)] = last[("prob_read", i)] = t
            tB[("o", b, m)] = t

        def o_copy(b, m):
            t = A(lambda e: e.copy(oT[:].rearrange("p a c -> p (a c)"), o_ps[:].rearrange("p a c -> p (a c)")),
                  tB[("o", b, m)], last.get("oT_read"))
            tB["oT"] = t

        def o_rows(b, m):
            t = PEq([lambda e, a=a: e.transpose(o_ps[:, a, :], oT[:, a, :], idn[:]) for a in range(HQ)], tB["oT"])
            last["oT_read"] = t
            heads = o_ps[:].rearrange("p a (h r) -> p (a h) r", r=VW)
            t = V(lambda e: e.reciprocal(rden[:].rearrange("p (h o) -> p h o", o=1), heads[:, :, HD:HD + 1]), t)
            tB["att"] = V(lambda e: e.tensor_tensor(att[:], heads[:, :, 0:HD],
                                                    rden[:].rearrange("p (h o) -> p h o", o=1).broadcast_to([P, H, HD]), ALU.mult),
                          t, last.get("att_read"))
            free["o"] = tB["att"]

        def o_columns(src):
            t = PEq([lambda e: e.transpose(v_ps[:, 0:P], src, idn[:])], tB["att"], free["v"])
            last["att_read"] = t
            free["v"] = tB["attT"] = A(lambda e: e.copy(attT[:], v_ps[:, 0:P]), t, last.get("attT_read"))

        def o_project(b, m):
            k, i = m // 2, b % NX
            t = PEq([lambda e: e.matmul(v_ps[:, 0:P], attT[:], wproj[:], start=True, stop=True)], tB["attT"], free["v"], w_att)
            last["attT_read"] = t
            t = V(lambda e: e.tensor_tensor(x2[b % N2][:, k, :], v_ps[:, 0:P], xpb[i][:, k, :], ALU.add), t,
                  tok_xpb[b], tok_store.get(b - N2))
            free["v"] = t
            last[("x2", b)] = t

        sC = {}

        def c_stats(b):
            sC["stats"] = norm_stats(x2[b % N2], stats2, mv2, veps2, rstd2, last[("x2", b)])

        def c_rows(b):
            sC["xn2"] = norm_rows(x2[b % N2], mv2, rstd2, xn2, sC["stats"], last.get("xn2_read"))

        def c_columns(b):
            last["xn2_read"], sC["xn2T"] = rows_to_columns(xn2, xn2T, sC["xn2"], last.get("xn2T_read"), last.get("route"))

        def c_split(b):
            sC["xn2hi"] = V(lambda e: e.tensor_copy(xn2hi[:], xn2T[:]), sC["xn2T"], last.get("xn2hi_read"))
            sC["xn2lo"] = last["xn2T_read"] = G(lambda e: e.tensor_tensor(xn2lo[:], xn2T[:], xn2hi[:].bitcast(F32), ALU.subtract),
                                                sC["xn2hi"], last.get("xn2hi_read"))

        def c_route(b, tiles):
            sC["route"] = PEq([lambda e, k=k: e.matmul(a_ps[:, k * E:(k + 1) * E], xn2T[:, k * P:(k + 1) * P], wrs[:],
                                                       start=True, stop=True) for k in tiles], sC["xn2T"], free["a"], w_exp)
            last["route"] = sC["route"]

        def c_logits(b):
            t = sC["route"]
            t = V(lambda e: e.tensor_tensor(logit[:], a_ps[:, 0:T * E].rearrange("p (t e) -> p t e", e=E),
                                            brs[:].rearrange("p (o e) -> p o e", o=1).broadcast_to([P, T, E]), ALU.add), t, w_exp)
            free["a"] = t
            t1 = V(lambda e: e.tensor_reduce(lmax[:], logit[:], AXX, ALU.max), t)
            mine = logit[:].rearrange("p t (e o) -> p t e o", o=1).broadcast_to([P, T, E, E])
            other = logit[:].rearrange("p t (o f) -> p t o f", o=1).broadcast_to([P, T, E, E])
            t2 = V(lambda e: e.tensor_tensor(level[:], other, mine, ALU.is_ge), t, last.get("before_read"))
            t3 = V(lambda e: e.tensor_tensor(before[:], other, mine, ALU.is_gt), t, last.get("before_read"))
            t1 = V(lambda e: e.tensor_tensor(gexp[:], logit[:], lmax[:].rearrange("p (t o) -> p t o", o=1).broadcast_to([P, T, E]),
                                             ALU.subtract), t1)
            sC["gexp"] = A(lambda e: e.activation(gexp[:], gexp[:], ACT.Exp), t1)
            t2 = V(lambda e: e.tensor_tensor(level[:], level[:], earlier[:], ALU.mult), t2, w_exp)
            t2 = V(lambda e: e.tensor_tensor(before[:], before[:], level[:], ALU.max), t2, t3)
            last["before_read"] = sC["beats"] = V(lambda e: e.tensor_reduce(beats[:], before[:], AXX, ALU.add), t2)

        def c_gates(b):
            t = V(lambda e: e.scalar_tensor_tensor(gexp[:], beats[:], 2.0, gexp[:], ALU.is_lt, ALU.mult), sC["beats"], sC["gexp"])
            t2 = V(lambda e: e.tensor_reduce(gsum[:], gexp[:], AXX, ALU.add), t)
            t2 = V(lambda e: e.reciprocal(gsum[:], gsum[:]), t2)
            sC[("gate", b)] = V(lambda e: e.tensor_tensor(gate[b % 2][:], gexp[:], gsum[:].rearrange("p (t o) -> p t o", o=1).broadcast_to([P, T, E]),
                                                     ALU.mult), t2, last.get(("gate_read", b % 2)))

        def c_gate_rows(b):
            t = PEq([lambda e, k=k: e.transpose(a_ps[0:E, k * P:(k + 1) * P], gate[b % 2][:, k, :], idn[:]) for k in range(T)],
                    sC[("gate", b)], free["a"])
            free["a"] = sC["gateT"] = A(lambda e: e.copy(gateT[:], a_ps[0:E, :]), t, last.get("gateT_read"))

        def c_constants(b):
            i = b % N2
            t = PEq([lambda e, k=k: e.matmul(a_ps[:, k * P:(k + 1) * P], gateT[:, k * P:(k + 1) * P], mexp[:],
                                             start=True, stop=True) for k in range(T)], sC["gateT"], free["a"], sE["m"])
            last["gateT_read"] = t
            t = V(lambda e: e.tensor_tensor(x2[i][:].rearrange("p t d -> p (t d)"), x2[i][:].rearrange("p t d -> p (t d)"),
                                            a_ps[:], ALU.add), t)
            free["a"] = t
            sC[("acc", b)] = [t] * T

        up_ps = [s_ps[0][:, 0:N], s_ps[0][:, N:], s_ps[1][:, 0:N], s_ps[1][:, N:]]

        down_ps = {"y": y_ps, "v": v_ps}
        UP_SPREAD = 3 * C

        def up_begin(b):
            sC["up"] = [free["s"][0], free["s"][0], free["s"][1], free["s"][1]]

        def c_up(b, k):
            x, c = k // C, k % C
            i = c if k < UP_SPREAD else 2 + k % 2
            hi, lo = w1hi[:, x, c * P:(c + 1) * P], w1lo[:, x, c * P:(c + 1) * P]
            t = PEq([lambda e: e.matmul(up_ps[i], hi, xn2hi[:], start=True, stop=False),
                     lambda e: e.matmul(up_ps[i], hi, xn2lo[:], start=False, stop=False),
                     lambda e: e.matmul(up_ps[i], lo, xn2hi[:], start=False, stop=True)],
                    sC["xn2hi"], sC["xn2lo"], sC["up"][i], sE["w1"])
            last["xn2hi_read"] = t
            sC["up"][i] = sC[("h", b, k)] = A(lambda e: e.activation(hid[:, k, :], up_ps[i], ACT.Gelu, bias=b1s[:, k:k + 1]),
                                              t, last.get(("hid_read", x)))
            free["s"][i // 2] = sC["up"][i]

        def c_down(b, x, k, bank="y"):
            i = b % N2
            y_ps = down_ps[bank]
            t = PEq([lambda e, c=c: e.matmul(y_ps[:, k * P:(k + 1) * P], hid[:, x * C + c, k * P:(k + 1) * P],
                                             w2s[:, x * C + c, :], start=(c == 0), stop=(c == C - 1))
                     for c in range(C)], sC[("h", b, x * C + C - 1)], free[bank])
            last[("hid_read", x)] = t
            sC[("acc", b)][k] = free[bank] = V(lambda e: e.scalar_tensor_tensor(
                x2[i][:, k, :], y_ps[:, k * P:(k + 1) * P], gate[b % 2][:, k, x:x + 1], x2[i][:, k, :], ALU.mult, ALU.add),
                t, sC[("acc", b)][k])

        def down_end(b, store, stored):
            last[("gate_read", b % 2)] = sC[("acc", b)][-1]
            tok_store[b] = run.put("sync", store, sC[("acc", b)], stored)

        def every_expert(b, before):
            up_begin(b)
            for x in range(E):
                before(x)
                for c in range(C):
                    c_up(b, x * C + c)
                if x >= 1:
                    for k in range(T):
                        c_down(b, x - 1, k, "yv"[k % 2])
            for k in range(T):
                c_down(b, E - 1, k, "yv"[k % 2])

        def store_of(b):
            return lambda e: e.dma_start(out[b].rearrange("(t p) d -> p t d", p=P), x2[b % N2][:]), out_done[b % N2]

        def general_select():
            for part, dst, total in ((0, gq, qsum), (1, gk, ksum)):
                t = project(part, 0)
                A(lambda e, dst=dst: e.copy(dst[:], a_ps[:]), t)
                sA["g"] = (run.act.sem, run.act.count)
                free["a"] = V(lambda e, total=total: e.tensor_reduce(
                    total[:], a_ps[:].rearrange("p (m s) -> p m s", s=BS), AXX, ALU.add), sA["g"])
            sA["qk"] = V(lambda e: e.tensor_tensor(
                qk[:], qsum[:].rearrange("p (m o) -> p m o", o=1).broadcast_to([P, M, M]),
                ksum[:].rearrange("p (o n) -> p o n", o=1).broadcast_to([P, M, M]), ALU.mult), free["a"])
            t = PEq([lambda e, k=k: e.matmul(y_ps[:, k * P:(k + 1) * P], xnT[:, k * P:(k + 1) * P], wqkv[:, 2 * D:],
                                             start=True, stop=True) for k in range(T)], sA["xnT"])
            sA["gv"] = free["y"] = A(lambda e: e.copy(gv[:].rearrange("p t d -> p (t d)"), y_ps[:]), t)
            a_products(0)
            t = best_blocks()
            t = V(lambda e: e.tensor_tensor(ceq[:], ceq[:], own[:], ALU.max), t)
            t = V(lambda e: e.tensor_scalar(ceq[:], ceq[:], -1.0, FAR, ALU.add, ALU.mult), t)
            t = PEq([lambda e: e.transpose(a_ps[0:M * M, 0:P], ceq[:].rearrange("p m n -> p (m n)"), idn[:])], t, free["a"])
            sA["bias"] = free["a"] = V(lambda e: e.tensor_copy(gbias[:], a_ps[0:M * M, 0:P]), t)

        def general_heads():
            read, filled, done = None, None, {}
            for h in range(H):
                tq = V(lambda e, h=h: e.tensor_scalar(gqh[:], gq[:], hmask[:, h:h + 1], None, ALU.mult), sA["g"], read)
                tb = V(lambda e, h=h: e.tensor_scalar(gbh[:], qrows[:], gbias[:, h * HD:h * HD + 1], None, ALU.mult),
                       sA["bias"], read)
                for k in range(T):
                    s = s_ps[0][:, 0:N]
                    read = PEq([lambda e, k=k: e.matmul(s, gqh[:, k * P:(k + 1) * P], gk[:], start=True, stop=False),
                                lambda e, k=k: e.matmul(s, gbh[:, k * P:(k + 1) * P], krows[:], start=False, stop=True)],
                               tq, tb, done.get("exp"))
                    t = V(lambda e: e.tensor_reduce(gmax[:], s, AXX, ALU.max, negate=True), read, done.get("exp"))
                    t = V(lambda e: e.tensor_scalar(gmax[:], gmax[:], SCALE, None, ALU.mult), t)
                    done["exp"] = A(lambda e: e.activation(gp[:], s, ACT.Exp, bias=gmax[:], scale=SCALE, accum_out=gsumr[:]),
                                    t, done.get("tr"), done.get("norm"))
                    done["tr"] = PEq([lambda e, c=c: e.transpose(s_ps[1][:, c * P:(c + 1) * P], gp[:, c * P:(c + 1) * P], idn[:])
                                      for c in range(T)], done["exp"], filled)
                    filled = A(lambda e: e.copy(gpT[:], s_ps[1][:, 0:N]), done["tr"], done.get("pv"))
                    done["pv"] = PEq([lambda e, c=c, h=h: e.matmul(v_ps[:, 0:HD], gpT[:, c * P:(c + 1) * P],
                                                                   gv[:, c, h * HD:(h + 1) * HD], start=(c == 0), stop=(c == T - 1))
                                      for c in range(T)], filled, sA["gv"], done.get("norm"))
                    t = V(lambda e: e.reciprocal(gsumr[:], gsumr[:]), done["exp"])
                    done["norm"] = V(lambda e, k=k, h=h: e.tensor_scalar(gatt[:, k, h * HD:(h + 1) * HD], v_ps[:, 0:HD], gsumr[:],
                                                                         None, ALU.mult), t, done["pv"])
            for k in range(T):
                tB["att"], free["v"] = done["norm"], free["v"] or done["norm"]
                o_columns(gatt[:, k, :])
                o_project(0, 2 * k)

        def stage_a(b):
            return {(0, 1): lambda: a_stats(b), (1, 1): lambda: a_rows(b), (1, 3): lambda: a_columns(b),
                    (2, 3): lambda: a_project_q(b), (3, 1): lambda: a_q(b),
                    (3, 3): lambda: (a_project_k(b), a_mask_q(b, (0, 1))), (4, 1): lambda: a_k(b),
                    (4, 3): lambda: (a_v(b), a_mask_q(b, (2, 3))), (5, 1): lambda: a_qk(b),
                    (5, 3): lambda: a_products(b), (6, 1): lambda: a_select(b)}

        def stage_c(b):
            return {(0, 2): lambda: c_columns(b), (0, 3): lambda: c_route(b, (0, 1)), (1, 2): lambda: (c_route(b, (2, 3)), c_logits(b)), (3, 3): lambda: c_split(b), (2, 1): lambda: c_gates(b),
                    (5, 2): lambda: c_gate_rows(b), (6, 3): lambda: c_constants(b)}

        def at(plans, m, place):
            for plan in plans:
                if (m, place) in plan:
                    plan[m, place]()

        def every(plan):
            for key in sorted(plan):
                plan[key]()

        def pair_columns():
            o_columns(att[:].rearrange("p h d -> p (h d)"))

        def begin(b):
            scores(b, 0)
            values(b, 0)
            block_max(b, 0)

        a_stats(0)
        a_rows(0)
        a_columns(0)
        tok_idn16 = V(lambda e: e.tensor_copy(idn16[:], idn[:]), w_in)
        a_project_q(0)
        a_q(0)
        a_project_k(0)
        a_mask_q(0, (0, 1))
        a_k(0)
        a_v(0)
        a_qk(0)
        a_mask_q(0, (2, 3))
        a_products(0)
        a_select(0)
        tok_hone = V(lambda e: e.tensor_copy(hone[:], hone32[:]), w_att)
        hidden_of_bias()
        expert_rows_sum()
        begin(0)
        for b in range(B):
            plans = []
            if b + 1 < B:
                plans.append(stage_a(b + 1))
            if b >= 1:
                plans.append(stage_c(b - 1))
            else:
                plans.append({(x, 3): lambda x=x: split_w1(x) for x in range(E)})
            down = [(b - 2, x, k) for x in range(E) for k in range(T)] if b >= 2 else []
            for m in range(M):
                if m >= 1:
                    weighted(b, m - 1)
                row_max(b, m)
                if m % 2 == 0 and m >= 2:
                    o_copy(b, m - 1)
                if down:
                    c_down(*down.pop(0))
                shift_exp(b, m)
                at(plans, m, 1)
                at(plans, m, 2)
                if m % 2 == 1 and m >= 3:
                    pair_columns()
                if m + 1 < M:
                    scores(b, m + 1)
                    block_max(b, m + 1)
                if m % 2 == 0 and m >= 4:
                    o_project(b, m - 3)
                if m % 2 == 0 and m >= 2:
                    o_rows(b, m - 1)
                if down:
                    c_down(*down.pop(0))
                if m + 1 < M:
                    values(b, m + 1)
                at(plans, m, 3)
            if b >= 2:
                down_end(b - 2, *store_of(b - 2))
            if b + 2 < B:
                load_x(b + 2)
            weighted(b, M - 1)
            o_project(b, M - 3)
            o_copy(b, M - 1)
            between = {1: lambda: o_rows(b, M - 1), 3: pair_columns, 5: lambda: o_project(b, M - 1),
                       7: lambda: c_stats(b), 9: lambda: c_rows(b)}
            if b + 1 < B:
                between[UP_SPREAD] = lambda: begin(b + 1)
            if b >= 1:
                up_begin(b - 1)
            for k in range(E * C):
                if b >= 1:
                    c_up(b - 1, k)
                if k in between:
                    between[k]()
        last_c = stage_c(B - 1)
        down = [(B - 2, x, k) for x in range(E) for k in range(T)]
        for key in sorted(last_c):
            last_c[key]()
            for _ in range(2):
                if down and down[0][1] < 1:
                    c_down(*down.pop(0))

        def expert_before(x):
            while down and down[0][1] <= x:
                c_down(*down[0], "yv"[down[0][2] % 2])
                down.pop(0)

        every_expert(B - 1, expert_before)
        down_end(B - 2, *store_of(B - 2))
        down_end(B - 1, *store_of(B - 1))
        for b in range(B - N2, B):
            run.put("sync", lambda e: e.nop(), [tok_store[b]])

        t = V(lambda e: e.tensor_reduce(tiemax[:], ties[:].rearrange("p b m -> p (b m)"), AXX, ALU.max), last["ties"])
        t = PEq([lambda e: e.transpose(a_ps[0:1, 0:P], tiemax[:], idn[:])], t, free["a"])
        t = V(lambda e: e.tensor_reduce(tieall[:], a_ps[0:1, 0:P], AXX, ALU.max), t)
        V(lambda e: e.tensor_scalar(tieflag[:], tieall[:], 1.5, None, ALU.is_gt), t)
        run.block(nc)

        tied = nc.values_load(tieflag[0:1, 0:1], min_val=0, max_val=1)
        with nc.If(tied > 0):
            with nc.Fori(0, B) as batch:
                run = Run(ev, "general")
                g_x, g_out = ev("g_x", 16), ev("g_out", 16)
                free = {"a": None, "v": None, "y": None, "o": None, "s": [None, None]}
                for d in (last, sA, tB, sC, tok_xpb, tok_xn, tok_store):
                    d.clear()
                tok_x[0] = run.put("sync", lambda e: e.dma_start(
                    xs[0][:], x[bass.ds(batch, 1)].rearrange("o (t p) d -> p (o t) d", p=P)), (), g_x)
                a_stats(0)
                a_rows(0)
                a_columns(0)
                general_select()
                general_heads()
                c_stats(0)
                c_rows(0)
                every(stage_c(0))
                every_expert(0, lambda x: None)
                down_end(0, lambda e: e.dma_start(
                    out[bass.ds(batch, 1)].rearrange("o (t p) d -> p (o t) d", p=P), x2[0][:]), g_out)
                run.put("sync", lambda e: e.nop(), [tok_store[0]])
                run.block(nc)
                nc.all_engine_barrier(sems_to_clear=range(run.dve.sem.num, g_out.sem.num + 1))


def constants():
    p = np.arange(P)
    f = np.float32
    head_one = np.zeros((H, H, P), f)
    head_one[np.arange(H), np.arange(H)] = 1
    expert_rows = np.zeros((P, E, C, E), f)
    expert_rows[:, np.arange(E), :, np.arange(E)] = 1
    return {
        "ident": np.eye(P, dtype=f),
        "quad_mask": (p[:, None] // HD % HQ == np.arange(HQ)).astype(f),
        "head_sum": (p[:, None] // HD == p // HD).astype(f),
        "head_one": head_one,
        "block_rank": np.broadcast_to((M - np.arange(M)).astype(f), (P, M, M)).copy(),
        "row_base": (p[:, None] * M + M).astype(f),
        "expert_before": np.broadcast_to((np.arange(E) < np.arange(E)[:, None]).astype(f), (P, T, E, E)).copy(),
        "expert_rows": expert_rows,
        "own_block": np.broadcast_to(np.eye(M, dtype=f), (P, M, M)).copy(),
        "head_mask": (p[:, None] // HD == np.arange(H)).astype(f),
        "query_rows": (np.arange(M * M)[:, None] // M == np.arange(N) // BS).astype(f),
        "key_rows": (np.arange(M * M)[:, None] % M == np.arange(N) // BS).astype(f),
    }


def kernel(**inputs):
    import concourse.bacc as bacc
    from concourse.bass_utils import run_bass_kernel_spmd

    a = {k: np.ascontiguousarray(v) for k, v in inputs.items()}
    arrays = {
        "x": a["L0_attn_x"],
        "wqkv_t": np.ascontiguousarray(a["L0_attn_qkv_w"].T),
        "wproj_t": np.ascontiguousarray(a["L0_attn_proj_w"].T),
        "proj_b": np.ascontiguousarray(np.broadcast_to(a["L0_attn_proj_b"], (P, D))),
        "w1": a["L0_ffn_w1"],
        "b1_t": np.ascontiguousarray(a["L0_ffn_b1"].reshape(E * C, P).T),
        "w2": a["L0_ffn_w2"],
        "b2": a["L0_ffn_b2"],
        "wr": a["L0_ffn_wr"],
        "br": np.ascontiguousarray(np.broadcast_to(a["L0_ffn_br"], (P, E))),
    } | constants()
    nc = bacc.Bacc("TRN2", target_bir_lowering=False, num_devices=1)
    args = {k: nc.dram_tensor(f"in_{k}", v.shape, mybir.dt.from_np(v.dtype), kind="ExternalInput").ap()
            for k, v in arrays.items()}
    out = nc.dram_tensor("out_x", (B, N, D), F32, kind="ExternalOutput").ap()
    layer(nc, **args, out=out)
    r = run_bass_kernel_spmd(nc, [{f"in_{k}": v for k, v in arrays.items()}], core_ids=[0])
    return r.results[0]["out_x"]
```

```python
from contextlib import ExitStack

import numpy as np

import concourse.bass as bass
from concourse import mybir

F32 = mybir.dt.float32
F32R = mybir.dt.float32r
BF16 = mybir.dt.bfloat16
U32 = mybir.dt.uint32
ALU = mybir.AluOpType
ACT = mybir.ActivationFunctionType
AXX = mybir.AxisListType.X

P = 128
B, N, D = 16, 512, 128
H = 16
HD = D // H
BS = 64
M = N // BS
T = N // P
SCALE = HD ** -0.5
EPS = 1e-5
E, HID = 4, 512
C = HID // P
QUADS = 4
HQ = H // QUADS
KEYS = 2 * BS
ROW = 3 * BS
FAR = 1e30
VW = 32


class Event:

    def __init__(self, sem, step=1):
        self.sem, self.step, self.count = sem, step, 0

    def tick(self):
        self.count += self.step
        return self.sem, self.count


class Run:

    def __init__(self, event, name):
        self.dve, self.pool, self.act, self.pe = (event(f"{name}_{e}") for e in ("dve", "pool", "act", "pe"))
        self.lists = {e: [] for e in ("sync", "gpsimd", "scalar", "vector", "tensor")}
        self.waited = {e: {} for e in self.lists}

    def put(self, engine, emit, after=(), done=None):
        waits = []
        for token in after:
            if token is None:
                continue
            sem, value = token
            if self.waited[engine].get(id(sem), 0) < value:
                self.waited[engine][id(sem)] = value
                waits.append(token)
        token = done.tick() if done else None
        self.lists[engine].append((waits, emit, done))
        return token

    def block(self, nc):
        with nc.Block() as block:
            block.sync(lambda eng: self.play("sync", eng))
            block.gpsimd(lambda eng: self.play("gpsimd", eng))
            block.scalar(lambda eng: self.play("scalar", eng))
            block.vector(lambda eng: self.play("vector", eng))
            block.tensor(lambda eng: self.play("tensor", eng))

    def play(self, engine, eng):
        for waits, emit, done in self.lists[engine]:
            for sem, value in waits:
                eng.wait_ge(sem, value)
            ins = emit(eng)
            if done:
                ins.then_inc(done.sem, done.step)


def layer(nc, x, wqkv_t, wproj_t, proj_b, w1, b1_t, w2, b2, wr, br, ident, quad_mask, head_sum,
          head_one, block_rank, row_base, expert_before, expert_rows, own_block, head_mask,
          query_rows, key_rows, out):
    with ExitStack() as ctx:
        def sb(name, shape, dt=F32):
            return ctx.enter_context(nc.sbuf_tensor(name, shape, dt))

        def ps(name, shape, dt=F32):
            return ctx.enter_context(nc.psum_tensor(name, shape, dt))

        def ev(name, step=1):
            return Event(ctx.enter_context(nc.semaphore(name)), step)

        wqkv = sb("wqkv", [P, 3 * D])
        wqkvhi, wqkvlo = sb("wqkvhi", [P, 3 * D], F32R), sb("wqkvlo", [P, 3 * D], F32R)
        wproj = sb("wproj", [P, D])
        projb = sb("projb", [P, D])
        w1hi, w1lo = sb("w1hi", [P, E, HID], F32R), sb("w1lo", [P, E, HID], F32R)
        w2s = sb("w2s", [P, E * C, D])
        b1s = sb("b1s", [P, E * C])
        b2s = sb("b2s", [E, D])
        wrs = sb("wrs", [P, E])
        brs = sb("brs", [P, E])
        idn = sb("idn", [P, P])
        qmask = sb("qmask", [P, HQ])
        hsum = sb("hsum", [P, P])
        hone32 = sb("hone32", [H, H, P])
        hone = sb("hone", [H, H, P], BF16)
        rank = sb("rank", [P, M, M])
        rbase = sb("rbase", [P, 1])
        erows = sb("erows", [P, E, C, E])
        neg_half = sb("neg_half", [P, T])
        ones4 = sb("ones4", [E, E])
        g1 = sb("g1", [P, E, C])
        g1m = sb("g1m", [P, E, C, E])
        cexp = sb("cexp", [E, D])
        mexp = sb("mexp", [E, D])

        NX, N2 = 2, 4
        xs = [sb(f"xs{i}", [P, T, D]) for i in range(NX)]
        xpb = [sb(f"xpb{i}", [P, T, D]) for i in range(NX)]
        x2 = [sb(f"x2{i}", [P, T, D]) for i in range(N2)]
        stats = sb("stats", [P, T, 6])
        mv = sb("mv", [P, T, 2])
        veps = sb("veps", [P, T])
        rstd = sb("rstd", [P, T])
        xn = sb("xn", [P, T, D])
        xnhi, xnlo = sb("xnhi", [P, N], F32R), sb("xnlo", [P, N], F32R)
        qhi = sb("qhi", [P, N], F32R)
        qlo = sb("qlo", [P, N])
        qmh = [sb(f"qmh{i}", [P, HQ, N], F32R) for i in range(2)]
        qml = [sb(f"qml{i}", [P, HQ, N], F32R) for i in range(2)]
        stage = [sb(f"stage{i}", [P, M, BS, 3], F32R) for i in range(2)]
        kv = [sb(f"kv{i}", [P, M, KEYS, 3], F32R) for i in range(2)]
        qsum = sb("qsum", [P, M])
        ksum = sb("ksum", [P, M])
        qk = sb("qk", [P, M, M])
        crow = sb("crow", [P, M, M])
        cmax = sb("cmax", [P, M])
        ceq = sb("ceq", [P, M, M])
        crank = sb("crank", [P, M, M])
        cbest = sb("cbest", [P, M])
        index = [sb(f"index{i}", [P, M], U32) for i in range(2)]
        ties = sb("ties", [P, B, M])
        vaug = [sb(f"vaug{i}", [P, H, VW]) for i in range(2)]
        rmax = [sb(f"rmax{i}", [P, H, 2], BF16) for i in range(2)]
        idn16 = sb("idn16", [P, P], BF16)
        nmax = [sb(f"nmax{i}", [H, BS], BF16) for i in range(2)]
        prob = [sb(f"prob{i}", [P, H, BS]) for i in range(2)]
        oT = sb("oT", [P, HQ, P])
        rden = sb("rden", [P, H])
        att = sb("att", [P, H, HD])
        attT = sb("attT", [P, P])
        stats2 = sb("stats2", [P, T, 6])
        mv2 = sb("mv2", [P, T, 2])
        veps2 = sb("veps2", [P, T])
        rstd2 = sb("rstd2", [P, T])
        xn2 = sb("xn2", [P, T, D])
        xn2T = sb("xn2T", [P, N])
        xn2hi, xn2lo = sb("xn2hi", [P, N], F32R), sb("xn2lo", [P, N], F32R)
        logit = sb("logit", [P, T, E])
        beats = sb("beats", [P, T, E])
        level, before = sb("level", [P, T, E, E]), sb("before", [P, T, E, E])
        earlier = sb("earlier", [P, T, E, E])
        lmax = sb("lmax", [P, T])
        gexp = sb("gexp", [P, T, E])
        gsum = sb("gsum", [P, T])
        gate = [sb(f"gate{i}", [P, T, E]) for i in range(2)]
        mcols = sb("mcols", [P, E, D])
        tiemax, tieall = sb("tiemax", [P, 1]), sb("tieall", [1, 1])
        tieflag = sb("tieflag", [1, 1], U32)
        own = sb("own", [P, M, M])
        hmask = sb("hmask", [P, H])
        qrows = sb("qrows", [M * M, N])
        krows = sb("krows", [M * M, N])
        gbias = sb("gbias", [M * M, P])
        gmax, gsumr = sb("gmax", [P, 1]), sb("gsumr", [P, 1])
        hid = sb("hid", [P, E * C, N])
        w1_landing = hid[:, 0:E, :]
        gq, gk, gqh, gbh, gp, gpT, gv, gatt = (hid[:, n, :] for n in range(8))
        gv, gatt = (r.rearrange("p (t d) -> p t d", d=D) for r in (gv, gatt))
        gbh = gbh[0:M * M, :]

        table = [nc.dram_tensor(f"kv_table{b}", [P * M, ROW], F32, kind="Internal").ap() for b in range(B)]

        s_ps = [ps(f"s_ps{i}", [P, 2 * N]) for i in range(2)]
        o_ps = ps("o_ps", [P, HQ, P])
        v_ps = ps("v_ps", [P, N])
        a_ps = ps("a_ps", [P, N])
        y_ps = ps("y_ps", [P, N])

        weights_in, attention_in, experts_in = (ev(name, 16) for name in ("weights_in", "attention_in", "experts_in"))
        x_in = [ev(f"x_in{i}", 16) for i in range(NX)]
        table_out = [ev(f"table_out{i}", 16) for i in range(2)]
        own_in = [ev(f"own_in{i}", 16) for i in range(2)]
        sel_in = [[ev(f"sel_in{i}_{m}", 16) for m in range(M)] for i in range(2)]
        out_done = [ev(f"out_done{i}", 16) for i in range(N2)]
        run = Run(ev, "fast")
        tok_x, tok_xpb, tok_xn, tok_store = {}, {}, {}, {}
        free = {"a": None, "v": None, "y": None, "o": None, "s": [None, None]}
        last, sA, sB, sC, sE = {}, {}, {}, {}, {}

        def V(emit, *after):
            return run.put("vector", emit, after, run.dve)

        def G(emit, *after):
            return run.put("gpsimd", emit, after, run.pool)

        def A(emit, *after):
            return run.put("scalar", emit, after, run.act)

        def PEq(emits, *after):
            for n, emit in enumerate(emits):
                token = run.put("tensor", emit, after if n == 0 else (), run.pe if n == len(emits) - 1 else None)
            return token

        first = [(idn, ident), (wqkv, wqkv_t), (projb, proj_b), (qmask, quad_mask)]
        second = [(hsum, head_sum), (rank, block_rank), (rbase, row_base), (hone32, head_one), (wproj, wproj_t)]
        third = [(b1s, b1_t), (w2s, w2.rearrange("e (c p) d -> p (e c) d", p=P)), (b2s, b2),
                 (earlier, expert_before), (erows, expert_rows),
                 (w1_landing, w1.rearrange("e d h -> d e h")), (wrs, wr), (brs, br), (own, own_block),
                 (hmask, head_mask), (qrows, query_rows), (krows, key_rows)]

        def load_x(b):
            i = b % NX
            tok_x[b] = run.put("sync", lambda e: e.dma_start(
                xs[i][:], x[b].rearrange("(t p) d -> p t d", p=P)),
                [tok_xpb.get(b - NX), tok_xn.get(b - NX)], x_in[i])

        def load(arrays, arrived):
            for dst, src in arrays:
                to = dst if isinstance(dst, bass.AP) else dst[:]
                token = run.put("sync", lambda e, to=to, src=src: e.dma_start(to, src), (), arrived)
            return token

        load_x(0)
        w_in = load(first, weights_in)
        w_att = load(second, attention_in)
        w_exp = load(third, experts_in)
        load_x(1)

        half_set = V(lambda e: e.memset(neg_half[:], -0.5))
        ones_set = V(lambda e: e.memset(ones4[:], 1.0))
        for i in range(2):
            t = V(lambda e, i=i: e.memset(vaug[i][:], 0.0))
        for i in range(2):
            vaug_set = V(lambda e, i=i: e.memset(vaug[i][:, :, HD:HD + 1], 1.0), t)

        def hidden_of_bias():
            t = A(lambda e: e.activation(g1[:], b1s[:].rearrange("p (e c) -> p e c", e=E), ACT.Gelu), w_exp)
            sE["g1m"] = V(lambda e: e.tensor_tensor(g1m[:], erows[:], g1[:].rearrange("p e (c o) -> p e c o", o=1).broadcast_to([P, E, C, E]),
                                                    ALU.mult), t, w_exp)

        def split_w1(x):
            t = G(lambda e: e.tensor_copy(w1hi[:, x, :], w1_landing[:, x, :]), w_exp)
            sE["w1"] = last[("hid_read", 0)] = G(lambda e: e.tensor_tensor(
                w1lo[:, x, :], w1_landing[:, x, :], w1hi[:, x, :].bitcast(F32), ALU.subtract), t)

        def expert_constants():
            t = PEq([lambda e, k=k: e.matmul(a_ps[0:E, 0:D], g1m[:, k // C, k % C, :], w2s[:, k, :],
                                             start=(k == 0), stop=(k == E * C - 1)) for k in range(E * C)], sE["g1m"], free["a"])
            t = V(lambda e: e.tensor_tensor(cexp[:], a_ps[0:E, 0:D], b2s[:], ALU.add), t)
            t = PEq([lambda e: e.matmul(a_ps[0:E, 0:D], ones4[:], cexp[:], start=True, stop=True)], t, ones_set)
            t = free["a"] = V(lambda e: e.tensor_tensor(mexp[:], a_ps[0:E, 0:D], cexp[:], ALU.subtract), t)
            t = V(lambda e: e.tensor_tensor(mexp[:], mexp[:], b2s[:], ALU.add), t)
            t = PEq([lambda e, x=x: e.matmul(a_ps[:, x * D:(x + 1) * D], hone32[0:E, x, :], mexp[:], start=True, stop=True)
                     for x in range(E)], t, w_att)
            free["a"] = sE["m"] = A(lambda e: e.copy(mcols[:].rearrange("p x d -> p (x d)"), a_ps[:]), t)

        def norm_stats(src, st, m_v, ve, rs, tok_src):
            for k in range(T):
                t = V(lambda e, k=k: e.bn_stats(st[:, k, :], src[:, k, :]), tok_src)
            for k in range(T):
                t2 = V(lambda e, k=k: e.bn_aggr(m_v[:, k, :], st[:, k, :]), t)
            t = G(lambda e: e.tensor_scalar(ve[:], m_v[:, :, 1], EPS, None, ALU.add), t2)
            return G(lambda e: e.tensor_tensor(rs[:], ve[:], neg_half[:], ALU.pow), t, half_set)

        def norm_rows(src, m_v, rs, dst, tok, free_dst):
            for k in range(T):
                t = V(lambda e, k=k: e.tensor_scalar(dst[:, k, :], src[:, k, :], m_v[:, k, 0:1],
                                                     rs[:, k:k + 1], ALU.subtract, ALU.mult), tok, free_dst)
            return t

        def rows_to_columns(src, tok):
            return PEq([lambda e, k=k: e.transpose(a_ps[:, k * P:(k + 1) * P], src[:, k, :], idn[:])
                        for k in range(T)], tok, free["a"], w_in)

        def exact(dst, left_hi, left_lo, right_hi, right_lo):
            return [lambda e: e.matmul(dst, left_hi, right_hi, start=True, stop=False),
                    lambda e: e.matmul(dst, left_hi, right_lo, start=False, stop=False),
                    lambda e: e.matmul(dst, left_lo, right_hi, start=False, stop=True)]

        def a_stats(b):
            sA["rstd"] = norm_stats(xs[b % NX], stats, mv, veps, rstd, tok_x[b])

        def a_rows(b):
            i = b % NX
            tok_xpb[b] = G(lambda e: e.tensor_tensor(
                xpb[i][:], xs[i][:], projb[:].rearrange("p (o d) -> p o d", o=1).broadcast_to([P, T, D]), ALU.add),
                tok_x[b], w_in, last.get(("x2", b - NX)))
            sA["xn"] = tok_xn[b] = norm_rows(xs[i], mv, rstd, xn, sA["rstd"], last.get("xn_read"))

        def a_columns(b):
            t = last["xn_read"] = rows_to_columns(xn, sA["xn"])
            hi = A(lambda e: e.copy(xnhi[:], a_ps[:]), t, last.get("xnT_read"))
            free["a"] = sA["xnT"] = V(lambda e: e.tensor_tensor(xnlo[:], a_ps[:], xnhi[:].bitcast(F32), ALU.subtract),
                                      hi, last.get("xnT_read"))

        banks = {"a": a_ps, "v": v_ps, "y": y_ps}

        def project(part, bank="a"):
            columns = slice(part * D, (part + 1) * D)
            last["xnT_read"] = PEq(exact(banks[bank][:], wqkvhi[:, columns], wqkvlo[:, columns], xnhi[:], xnlo[:]),
                                   sA["xnT"], free[bank], w_qkv)
            return last["xnT_read"]

        def a_project_q(b):
            sA["q_ps"] = project(0)

        def a_q(b):
            t = sA["q_ps"]
            sA["qhi"] = V(lambda e: e.tensor_copy(qhi[:], a_ps[:]), t, last.get("qhi_read"))
            V(lambda e: e.tensor_reduce(qsum[:], a_ps[:].rearrange("p (m s) -> p m s", s=BS), AXX, ALU.add), t)
            sA["qlo"] = free["a"] = V(lambda e: e.tensor_tensor(qlo[:], a_ps[:], qhi[:].bitcast(F32), ALU.subtract),
                                      sA["qhi"], last.get("qlo_read"))

        def a_mask_q(b, heads):
            j = b % 2
            for h in heads:
                last["qhi_read"] = V(lambda e, h=h: e.tensor_scalar(qmh[j][:, h, :], qhi[:].bitcast(F32), qmask[:, h:h + 1],
                                                                    None, ALU.mult), sA["qhi"], w_in, last.get(("q_read", j)))
                last["qlo_read"] = G(lambda e, h=h: e.tensor_scalar(qml[j][:, h, :], qlo[:], qmask[:, h:h + 1],
                                                                    1.0, ALU.mult, ALU.mult), sA["qlo"], w_in, last.get(("q_read", j)))
            sA[("q", b)] = (last["qhi_read"], last["qlo_read"])

        def a_project_k(b, bank="a"):
            sA["k_ps"] = project(1, bank)

        def a_k(b, bank="a"):
            j = b % 2
            st = stage[j]
            kview = banks[bank][:].rearrange("p (m s) -> p m s", s=BS)
            hi = V(lambda e: e.tensor_copy(st[:, :, :, 0], kview), sA["k_ps"], last.get(("stage_read", j)), last.get(("stage_read2", j)))
            V(lambda e: e.tensor_reduce(ksum[:], kview, AXX, ALU.add), sA["k_ps"])
            sA["k"] = free[bank] = V(lambda e: e.tensor_tensor(st[:, :, :, 1], kview, st[:, :, :, 0].bitcast(F32),
                                                               ALU.subtract), hi)

        def a_qk(b):
            sA["qk"] = V(lambda e: e.tensor_tensor(
                qk[:], qsum[:].rearrange("p (m o) -> p m o", o=1).broadcast_to([P, M, M]),
                ksum[:].rearrange("p (o n) -> p o n", o=1).broadcast_to([P, M, M]), ALU.mult), sA["k"])

        def a_v(b, bank="a"):
            j = b % 2
            st = stage[j]
            t = project(2, bank)
            free[bank] = A(lambda e: e.copy(st[:, :, :, 2].bitcast(F32), banks[bank][:].rearrange("p (m s) -> p m s", s=BS)),
                          t, last.get(("stage_read", j)), last.get(("stage_read2", j)))
            tb = run.put("sync", lambda e: e.dma_start(
                table[b][:, :].rearrange("(p n) c -> p (n c)", n=M), st[:].bitcast(F32).rearrange("p n s c -> p (n s c)")),
                [free[bank], sA["k"]], table_out[j])
            own_t = run.put("sync", lambda e: e.dma_start(
                kv[j][:, :, 0:BS, :].bitcast(F32).rearrange("p m s c -> p m (s c)"), st[:].bitcast(F32).rearrange("p m s c -> p m (s c)")),
                [last.get(("kv_read", j))], own_in[j])
            last[("stage_read", j)], last[("stage_read2", j)] = tb, own_t
            sA[("own", b)] = own_t
            sA["table"] = tb

        def a_products(b):
            sA["c_ps"] = PEq([lambda e: e.matmul(a_ps[:, 0:M * M], hsum[:], qk[:].rearrange("p m n -> p (m n)"),
                                        start=True, stop=True)], sA["qk"], free["a"], w_att)

        def best_blocks():
            t = V(lambda e: e.tensor_scalar(crow[:].rearrange("p m n -> p (m n)"), a_ps[:, 0:M * M],
                                            1.0 / (BS * BS), SCALE, ALU.mult, ALU.mult), sA["c_ps"])
            free["a"] = t
            t = V(lambda e: e.tensor_reduce(cmax[:], crow[:], AXX, ALU.max), t)
            return V(lambda e: e.tensor_tensor(ceq[:], crow[:], cmax[:].rearrange("p (m o) -> p m o", o=1).broadcast_to([P, M, M]),
                                               ALU.is_ge), t)

        def a_select(b):
            j = b % 2
            t = best_blocks()
            last["ties"] = V(lambda e: e.tensor_reduce(ties[:, b, :], ceq[:], AXX, ALU.add), t)
            t = V(lambda e: e.tensor_tensor(crank[:], ceq[:], rank[:], ALU.mult), t, w_att)
            t = V(lambda e: e.tensor_reduce(cbest[:], crank[:], AXX, ALU.max), t)
            t = V(lambda e: e.tensor_scalar(index[j][:], cbest[:], -1.0, rbase[:], ALU.mult, ALU.add), t,
                  *(sA.get(("sel", b - 2, m)) for m in range(M)))
            for m in range(M):
                g = run.put("gpsimd", lambda e, m=m: e.indirect_dma_start(
                    out=kv[j][:, m, BS:, :].bitcast(F32).rearrange("p s c -> p (s c)"), out_offset=None, in_=table[b][:, :],
                    in_offset=bass.IndirectOffsetOnAxis(ap=index[j][:, m:m + 1], axis=0)),
                    [t, sA["table"], last.get(("kv_read", j))], sel_in[j][m])
                sA[("sel", b, m)] = g

        def scores(b, m):
            j, i = b % 2, m % 2
            keys_hi = kv[j][:, m, :, 0]
            keys_lo = kv[j][:, m, :, 1]
            halves = []
            for g, bank_first in ((0, True), (2, True), (1, False), (3, False)):
                r = slice(32 * g, 32 * g + 32)
                dst = s_ps[i][:, g * HQ * BS:(g + 1) * HQ * BS].rearrange("p (h s) -> p h s", s=BS)
                qh = qmh[j][r, :, m * BS:(m + 1) * BS]
                ql = qml[j][r, :, m * BS:(m + 1) * BS]
                emits = [lambda e, l=l, rr=rr, s=s, dst=dst: e.matmul(dst, l, rr, start=s, stop=False, skip_group_check=True)
                         for l, rr, s in ((keys_hi[r], qh, bank_first), (keys_hi[r], ql, False), (keys_lo[r], qh, False))]
                halves.append(PEq(emits, halves[-2] if len(halves) >= 2 else None, *sA[("q", b)], sA[("own", b)],
                                  sA[("sel", b, m)], free["s"][i]))
            sB[("s", b, m)] = halves[2], halves[3]
            last[("q_read", j)] = halves[3]

        def values(b, m):
            j, i = b % 2, m % 2
            t = PEq([lambda e: e.transpose(v_ps[:, 0:P], kv[j][:, m, :, 2].bitcast(F32), idn[:])],
                    sA[("own", b)], sA[("sel", b, m)], free["v"])
            last[("kv_read", j)] = t
            t = A(lambda e: e.copy(vaug[i][:, :, 0:HD], v_ps[:, 0:P].rearrange("p (h d) -> p h d", d=HD)), t, vaug_set,
                  last.get(("vaug_read", i)))
            free["v"] = t
            sB[("v", b, m)] = t

        def block_max(b, m):
            i = m % 2
            for half in range(2):
                t = V(lambda e, half=half: e.tensor_reduce(
                    rmax[i][:, half * 8:(half + 1) * 8, :],
                    s_ps[i][:, half * N:(half + 1) * N].rearrange("p (a c) -> p a c", c=32), AXX, ALU.max,
                    apply_transpose=True), sB[("s", b, m)][half], last.get(("rmax_read", i)))
            sB[("rmax", b, m)] = t

        def row_max(b, m):
            i = m % 2
            t = PEq([lambda e, k=k: e.transpose(v_ps[0:H, k * P // 2:(k + 1) * P // 2].bitcast(BF16), rmax[i][:, :, k],
                                                idn16[:]) for k in range(2)],
                    sB[("rmax", b, m)], free["v"], idn16_ready)
            last[("rmax_read", i)] = t
            t = V(lambda e: e.tensor_reduce(
                nmax[i][:].rearrange("h (b c) -> h b c", b=2),
                v_ps[0:H, 0:P].bitcast(BF16).rearrange("h (b g c) -> h b c g", b=2, g=4), AXX, ALU.max, negate=True), t,
                last.get(("nmax_read", i)))
            free["v"] = t
            sB[("nmax", b, m)] = t

        def shift_exp(b, m):
            i = m % 2
            t = PEq([lambda e, h=h: e.matmul(s_ps[i][:, h * BS:(h + 1) * BS], hone[:, h, :], nmax[i][:],
                                             start=False, stop=True, skip_group_check=True) for h in range(H)],
                    sB[("nmax", b, m)], *sB[("s", b, m)], hone_ready)
            last[("nmax_read", i)] = t
            t = A(lambda e: e.activation(prob[i][:].rearrange("p h s -> p (h s)"), s_ps[i][:], ACT.Exp, scale=SCALE), t,
                  last.get(("prob_read", i)))
            free["s"][i] = t
            sB[("p", b, m)] = t

        def weighted(b, m):
            i = m % 2
            t = PEq([lambda e, h=h: e.matmul(o_ps[32 * (h % HQ):32 * (h % HQ) + VW, h // HQ, i * BS:(i + 1) * BS],
                                             vaug[i][:, h, :], prob[i][:, h, :], start=True, stop=True)
                     for h in range(H)], sB[("p", b, m)], sB[("v", b, m)], free["o"] if i == 0 else None)
            last[("vaug_read", i)] = last[("prob_read", i)] = t
            sB[("o", b, m)] = t

        def o_copy(b, m):
            t = A(lambda e: e.copy(oT[:].rearrange("p a c -> p (a c)"), o_ps[:].rearrange("p a c -> p (a c)")),
                  sB[("o", b, m)], last.get("oT_read"))
            sB["oT"] = t

        def o_rows(b, m):
            t = PEq([lambda e, a=a: e.transpose(o_ps[:, a, :], oT[:, a, :], idn[:]) for a in range(HQ)], sB["oT"])
            last["oT_read"] = t
            heads = o_ps[:].rearrange("p a (h r) -> p (a h) r", r=VW)
            t = V(lambda e: e.reciprocal(rden[:].rearrange("p (h o) -> p h o", o=1), heads[:, :, HD:HD + 1]), t)
            sB["att"] = V(lambda e: e.tensor_tensor(att[:], heads[:, :, 0:HD],
                                                    rden[:].rearrange("p (h o) -> p h o", o=1).broadcast_to([P, H, HD]), ALU.mult),
                          t, last.get("att_read"))
            free["o"] = sB["att"]

        def o_columns(src):
            t = PEq([lambda e: e.transpose(v_ps[:, 0:P], src, idn[:])], sB["att"], free["v"])
            last["att_read"] = t
            free["v"] = sB["attT"] = A(lambda e: e.copy(attT[:], v_ps[:, 0:P]), t, last.get("attT_read"))

        def o_project(b, m):
            k, i = m // 2, b % NX
            t = PEq([lambda e: e.matmul(v_ps[:, 0:P], attT[:], wproj[:], start=True, stop=True)], sB["attT"], free["v"], w_att)
            last["attT_read"] = t
            t = V(lambda e: e.tensor_tensor(x2[b % N2][:, k, :], v_ps[:, 0:P], xpb[i][:, k, :], ALU.add), t,
                  tok_xpb[b], tok_store.get(b - N2))
            free["v"] = t
            last[("x2", b)] = t

        def c_stats(b):
            sC["stats"] = norm_stats(x2[b % N2], stats2, mv2, veps2, rstd2, last[("x2", b)])

        def c_rows(b):
            sC["xn2"] = norm_rows(x2[b % N2], mv2, rstd2, xn2, sC["stats"], last.get("xn2_read"))

        def c_columns(b):
            t = last["xn2_read"] = rows_to_columns(xn2, sC["xn2"])
            free["a"] = sC["xn2T"] = A(lambda e: e.copy(xn2T[:], a_ps[:]), t, last.get("xn2T_read"), last.get("route"))

        def c_split(b):
            sC["xn2hi"] = V(lambda e: e.tensor_copy(xn2hi[:], xn2T[:]), sC["xn2T"], last.get("xn2hi_read"))
            sC["xn2lo"] = last["xn2T_read"] = G(lambda e: e.tensor_tensor(xn2lo[:], xn2T[:], xn2hi[:].bitcast(F32), ALU.subtract),
                                                sC["xn2hi"], last.get("xn2hi_read"))

        def c_route(b, tiles):
            sC["route"] = PEq([lambda e, k=k: e.matmul(a_ps[:, k * E:(k + 1) * E], xn2T[:, k * P:(k + 1) * P], wrs[:],
                                                       start=True, stop=True) for k in tiles], sC["xn2T"], free["a"], w_exp)
            last["route"] = sC["route"]

        def c_logits(b):
            t = sC["route"]
            t = V(lambda e: e.tensor_tensor(logit[:], a_ps[:, 0:T * E].rearrange("p (t e) -> p t e", e=E),
                                            brs[:].rearrange("p (o e) -> p o e", o=1).broadcast_to([P, T, E]), ALU.add), t, w_exp)
            free["a"] = t
            t1 = V(lambda e: e.tensor_reduce(lmax[:], logit[:], AXX, ALU.max), t)
            mine = logit[:].rearrange("p t (e o) -> p t e o", o=1).broadcast_to([P, T, E, E])
            other = logit[:].rearrange("p t (o f) -> p t o f", o=1).broadcast_to([P, T, E, E])
            t2 = V(lambda e: e.tensor_tensor(level[:], other, mine, ALU.is_ge), t, last.get("before_read"))
            t3 = V(lambda e: e.tensor_tensor(before[:], other, mine, ALU.is_gt), t, last.get("before_read"))
            t1 = V(lambda e: e.tensor_tensor(gexp[:], logit[:], lmax[:].rearrange("p (t o) -> p t o", o=1).broadcast_to([P, T, E]),
                                             ALU.subtract), t1)
            sC["gexp"] = A(lambda e: e.activation(gexp[:], gexp[:], ACT.Exp), t1)
            t2 = V(lambda e: e.tensor_tensor(level[:], level[:], earlier[:], ALU.mult), t2, w_exp)
            t2 = V(lambda e: e.tensor_tensor(before[:], before[:], level[:], ALU.max), t2, t3)
            last["before_read"] = sC["beats"] = V(lambda e: e.tensor_reduce(beats[:], before[:], AXX, ALU.add), t2)

        def c_gates(b):
            t = V(lambda e: e.scalar_tensor_tensor(gexp[:], beats[:], 2.0, gexp[:], ALU.is_lt, ALU.mult), sC["beats"], sC["gexp"])
            t2 = V(lambda e: e.tensor_reduce(gsum[:], gexp[:], AXX, ALU.add), t)
            t2 = V(lambda e: e.reciprocal(gsum[:], gsum[:]), t2)
            sC[("gate", b)] = V(lambda e: e.tensor_tensor(gate[b % 2][:], gexp[:], gsum[:].rearrange("p (t o) -> p t o", o=1).broadcast_to([P, T, E]),
                                                     ALU.mult), t2, last.get(("gate_read", b % 2)))

        def c_constants(b, experts):
            i = b % N2
            acc = sC.setdefault(("acc", b), [None] * T)
            for x in experts:
                for k in range(T):
                    acc[k] = V(lambda e, x=x, k=k: e.scalar_tensor_tensor(
                        x2[i][:, k, :], mcols[:, x, :], gate[b % 2][:, k, x:x + 1], x2[i][:, k, :], ALU.mult, ALU.add),
                        acc[k], sC[("gate", b)], sE["m"], sC["xn2"])

        up_ps = [s_ps[0][:, 0:N], s_ps[0][:, N:], s_ps[1][:, 0:N], s_ps[1][:, N:]]

        UP_SPREAD = 3 * C + 1

        def up_begin(b):
            sC["up"] = [free["s"][0], free["s"][0], free["s"][1], free["s"][1]]

        def c_up(b, k):
            x, c = k // C, k % C
            i = c if k < UP_SPREAD else 2 + k % 2
            hi, lo = w1hi[:, x, c * P:(c + 1) * P], w1lo[:, x, c * P:(c + 1) * P]
            t = PEq(exact(up_ps[i], hi, lo, xn2hi[:], xn2lo[:]), sC["xn2hi"], sC["xn2lo"], sC["up"][i], sE["w1"])
            last["xn2hi_read"] = t
            sC["up"][i] = sC[("h", b, k)] = A(lambda e: e.activation(hid[:, k, :], up_ps[i], ACT.Gelu, bias=b1s[:, k:k + 1]),
                                              t, last.get(("hid_read", x)))
            free["s"][i // 2] = sC["up"][i]

        def c_down(b, x, k, bank="y"):
            i = b % N2
            y_ps = banks[bank]
            t = PEq([lambda e, c=c: e.matmul(y_ps[:, k * P:(k + 1) * P], hid[:, x * C + c, k * P:(k + 1) * P],
                                             w2s[:, x * C + c, :], start=(c == 0), stop=(c == C - 1))
                     for c in range(C)], sC[("h", b, x * C + C - 1)], free[bank])
            last[("hid_read", x)] = t
            sC[("acc", b)][k] = free[bank] = V(lambda e: e.scalar_tensor_tensor(
                x2[i][:, k, :], y_ps[:, k * P:(k + 1) * P], gate[b % 2][:, k, x:x + 1], x2[i][:, k, :], ALU.mult, ALU.add),
                t, sC[("acc", b)][k])

        def down_end(b, store, stored):
            last[("gate_read", b % 2)] = sC[("acc", b)][-1]
            tok_store[b] = run.put("sync", store, sC[("acc", b)], stored)

        def every_expert(b, before):
            up_begin(b)
            for x in range(E):
                before(x)
                for c in range(C):
                    c_up(b, x * C + c)
                if x >= 1:
                    for k in range(T):
                        c_down(b, x - 1, k, "yv"[k % 2])
            for k in range(T):
                c_down(b, E - 1, k, "yv"[k % 2])

        def store_of(b):
            return lambda e: e.dma_start(out[b].rearrange("(t p) d -> p t d", p=P), x2[b % N2][:]), out_done[b % N2]

        def general_select():
            for part, dst, total in ((0, gq, qsum), (1, gk, ksum)):
                t = project(part)
                A(lambda e, dst=dst: e.copy(dst[:], a_ps[:]), t)
                sA["g"] = (run.act.sem, run.act.count)
                free["a"] = V(lambda e, total=total: e.tensor_reduce(
                    total[:], a_ps[:].rearrange("p (m s) -> p m s", s=BS), AXX, ALU.add), sA["g"])
            sA["qk"] = V(lambda e: e.tensor_tensor(
                qk[:], qsum[:].rearrange("p (m o) -> p m o", o=1).broadcast_to([P, M, M]),
                ksum[:].rearrange("p (o n) -> p o n", o=1).broadcast_to([P, M, M]), ALU.mult), free["a"])
            t = PEq([emit for k in range(T) for emit in exact(
                y_ps[:, k * P:(k + 1) * P], xnhi[:, k * P:(k + 1) * P], xnlo[:, k * P:(k + 1) * P],
                wqkvhi[:, 2 * D:], wqkvlo[:, 2 * D:])], sA["xnT"])
            sA["gv"] = free["y"] = A(lambda e: e.copy(gv[:].rearrange("p t d -> p (t d)"), y_ps[:]), t)
            a_products(0)
            t = best_blocks()
            t = V(lambda e: e.tensor_tensor(ceq[:], ceq[:], own[:], ALU.max), t)
            t = V(lambda e: e.tensor_scalar(ceq[:], ceq[:], -1.0, FAR, ALU.add, ALU.mult), t)
            t = PEq([lambda e: e.transpose(a_ps[0:M * M, 0:P], ceq[:].rearrange("p m n -> p (m n)"), idn[:])], t, free["a"])
            sA["bias"] = free["a"] = V(lambda e: e.tensor_copy(gbias[:], a_ps[0:M * M, 0:P]), t)

        def general_heads():
            read, filled, done = None, None, {}
            for h in range(H):
                tq = V(lambda e, h=h: e.tensor_scalar(gqh[:], gq[:], hmask[:, h:h + 1], None, ALU.mult), sA["g"], read)
                tb = V(lambda e, h=h: e.tensor_scalar(gbh[:], qrows[:], gbias[:, h * HD:h * HD + 1], None, ALU.mult),
                       sA["bias"], read)
                for k in range(T):
                    s = s_ps[0][:, 0:N]
                    read = PEq([lambda e, k=k: e.matmul(s, gqh[:, k * P:(k + 1) * P], gk[:], start=True, stop=False),
                                lambda e, k=k: e.matmul(s, gbh[:, k * P:(k + 1) * P], krows[:], start=False, stop=True)],
                               tq, tb, done.get("exp"))
                    t = V(lambda e: e.tensor_reduce(gmax[:], s, AXX, ALU.max, negate=True), read, done.get("exp"))
                    t = V(lambda e: e.tensor_scalar(gmax[:], gmax[:], SCALE, None, ALU.mult), t)
                    done["exp"] = A(lambda e: e.activation(gp[:], s, ACT.Exp, bias=gmax[:], scale=SCALE, accum_out=gsumr[:]),
                                    t, done.get("tr"), done.get("norm"))
                    done["tr"] = PEq([lambda e, c=c: e.transpose(s_ps[1][:, c * P:(c + 1) * P], gp[:, c * P:(c + 1) * P], idn[:])
                                      for c in range(T)], done["exp"], filled)
                    filled = A(lambda e: e.copy(gpT[:], s_ps[1][:, 0:N]), done["tr"], done.get("pv"))
                    done["pv"] = PEq([lambda e, c=c, h=h: e.matmul(v_ps[:, 0:HD], gpT[:, c * P:(c + 1) * P],
                                                                   gv[:, c, h * HD:(h + 1) * HD], start=(c == 0), stop=(c == T - 1))
                                      for c in range(T)], filled, sA["gv"], done.get("norm"))
                    t = V(lambda e: e.reciprocal(gsumr[:], gsumr[:]), done["exp"])
                    done["norm"] = V(lambda e, k=k, h=h: e.tensor_scalar(gatt[:, k, h * HD:(h + 1) * HD], v_ps[:, 0:HD], gsumr[:],
                                                                         None, ALU.mult), t, done["pv"])
            for k in range(T):
                sB["att"], free["v"] = done["norm"], free["v"] or done["norm"]
                o_columns(gatt[:, k, :])
                o_project(0, 2 * k)

        def stage_a(b):
            return {(0, 1): lambda: a_stats(b), (1, 1): lambda: a_rows(b), (1, 3): lambda: a_columns(b),
                    (2, 3): lambda: a_project_q(b), (3, 1): lambda: a_q(b),
                    (3, 3): lambda: (a_project_k(b), a_mask_q(b, (0, 1))), (4, 1): lambda: a_k(b),
                    (4, 3): lambda: (a_v(b), a_mask_q(b, (2, 3))), (5, 1): lambda: a_qk(b),
                    (5, 3): lambda: a_products(b), (6, 1): lambda: a_select(b)}

        def stage_c(b):
            return {(0, 2): lambda: c_columns(b), (0, 3): lambda: c_route(b, (0, 1)),
                    (1, 2): lambda: (c_route(b, (2, 3)), c_logits(b)), (2, 1): lambda: c_gates(b), (3, 3): lambda: c_split(b),
                    (5, 1): lambda: c_constants(b, (0, 1)), (7, 1): lambda: c_constants(b, (2, 3))}

        def at(plans, m, place):
            for plan in plans:
                if (m, place) in plan:
                    plan[m, place]()

        def every(plan):
            for key in sorted(plan):
                plan[key]()

        def pair_columns():
            o_columns(att[:].rearrange("p h d -> p (h d)"))

        def begin(b):
            scores(b, 0)
            values(b, 0)
            block_max(b, 0)

        a_stats(0)
        t = V(lambda e: e.tensor_copy(wqkvhi[:], wqkv[:]), w_in)
        w_qkv = V(lambda e: e.tensor_tensor(wqkvlo[:], wqkv[:], wqkvhi[:].bitcast(F32), ALU.subtract), t)
        a_rows(0)
        a_columns(0)
        idn16_ready = V(lambda e: e.tensor_copy(idn16[:], idn[:]), w_in)
        a_project_q(0)
        a_project_k(0, "y")
        a_q(0)
        a_k(0, "y")
        a_v(0, "v")
        a_qk(0)
        a_mask_q(0, range(HQ))
        a_products(0)
        a_select(0)
        hone_ready = V(lambda e: e.tensor_copy(hone[:], hone32[:]), w_att)
        hidden_of_bias()
        expert_constants()
        begin(0)
        for b in range(B):
            plans = []
            if b + 1 < B:
                plans.append(stage_a(b + 1))
            if b >= 1:
                plans.append(stage_c(b - 1))
            else:
                plans.append({(x, 3): lambda x=x: split_w1(x) for x in range(E)})
            down = [(b - 2, x, k) for x in range(E) for k in range(T)] if b >= 2 else []
            for m in range(M):
                pv_first = bool(down)
                if m >= 1 and pv_first:
                    weighted(b, m - 1)
                row_max(b, m)
                if m >= 1 and not pv_first:
                    weighted(b, m - 1)
                if m % 2 == 0 and m >= 2:
                    o_copy(b, m - 1)
                if down:
                    c_down(*down.pop(0))
                shift_exp(b, m)
                at(plans, m, 1)
                at(plans, m, 2)
                if m % 2 == 1 and m >= 3:
                    pair_columns()
                if m + 1 < M:
                    scores(b, m + 1)
                    block_max(b, m + 1)
                if m % 2 == 0 and m >= 4:
                    o_project(b, m - 3)
                if m % 2 == 0 and m >= 2:
                    o_rows(b, m - 1)
                if down:
                    c_down(*down.pop(0))
                if m + 1 < M:
                    values(b, m + 1)
                at(plans, m, 3)
            if b >= 2:
                down_end(b - 2, *store_of(b - 2))
            if b + 2 < B:
                load_x(b + 2)
            weighted(b, M - 1)
            o_project(b, M - 3)
            o_copy(b, M - 1)
            between = {1: lambda: o_rows(b, M - 1), 3: pair_columns, 5: lambda: o_project(b, M - 1),
                       7: lambda: c_stats(b), 9: lambda: c_rows(b)}
            if b + 1 < B:
                between[UP_SPREAD if b >= 1 else 0] = lambda: begin(b + 1)
            if b >= 1:
                up_begin(b - 1)
            for k in range(E * C):
                if b >= 1:
                    c_up(b - 1, k)
                if k in between:
                    between[k]()
        last_c = stage_c(B - 1)
        down = [(B - 2, x, k) for x in range(E) for k in range(T)]

        def down_next():
            b, x, k = down.pop(0)
            c_down(b, x, k, "yv"[k % 2])

        def expert_before(x):
            while down and down[0][1] <= x:
                down_next()

        for key in sorted(last_c, key=lambda key: (key != (0, 2), key != (3, 3), key)):
            last_c[key]()
            for _ in range(2):
                if down[0][1] < 2:
                    down_next()

        every_expert(B - 1, expert_before)
        down_end(B - 2, *store_of(B - 2))
        down_end(B - 1, *store_of(B - 1))
        for b in range(B - N2, B):
            run.put("sync", lambda e: e.nop(), [tok_store[b]])

        t = V(lambda e: e.tensor_reduce(tiemax[:], ties[:].rearrange("p b m -> p (b m)"), AXX, ALU.max), last["ties"])
        t = PEq([lambda e: e.transpose(a_ps[0:1, 0:P], tiemax[:], idn[:])], t, free["a"])
        t = V(lambda e: e.tensor_reduce(tieall[:], a_ps[0:1, 0:P], AXX, ALU.max), t)
        V(lambda e: e.tensor_scalar(tieflag[:], tieall[:], 1.5, None, ALU.is_gt), t)
        run.block(nc)

        tied = nc.values_load(tieflag[0:1, 0:1], min_val=0, max_val=1)
        with nc.If(tied > 0):
            with nc.Fori(0, B) as batch:
                run = Run(ev, "general")
                g_x, g_out = ev("g_x", 16), ev("g_out", 16)
                free = {"a": None, "v": None, "y": None, "o": None, "s": [None, None]}
                for d in (last, sA, sB, sC, tok_xpb, tok_xn, tok_store):
                    d.clear()
                tok_x[0] = run.put("sync", lambda e: e.dma_start(
                    xs[0][:], x[bass.ds(batch, 1)].rearrange("o (t p) d -> p (o t) d", p=P)), (), g_x)
                a_stats(0)
                a_rows(0)
                a_columns(0)
                general_select()
                general_heads()
                c_stats(0)
                c_rows(0)
                every(stage_c(0))
                every_expert(0, lambda x: None)
                down_end(0, lambda e: e.dma_start(
                    out[bass.ds(batch, 1)].rearrange("o (t p) d -> p (o t) d", p=P), x2[0][:]), g_out)
                run.put("sync", lambda e: e.nop(), [tok_store[0]])
                run.block(nc)
                nc.all_engine_barrier(sems_to_clear=range(run.dve.sem.num, g_out.sem.num + 1))


def constants():
    p = np.arange(P)
    f = np.float32
    head_one = np.zeros((H, H, P), f)
    head_one[np.arange(H), np.arange(H)] = 1
    expert_rows = np.zeros((P, E, C, E), f)
    expert_rows[:, np.arange(E), :, np.arange(E)] = 1
    return {
        "ident": np.eye(P, dtype=f),
        "quad_mask": (p[:, None] // HD % HQ == np.arange(HQ)).astype(f),
        "head_sum": (p[:, None] // HD == p // HD).astype(f),
        "head_one": head_one,
        "block_rank": np.broadcast_to((M - np.arange(M)).astype(f), (P, M, M)).copy(),
        "row_base": (p[:, None] * M + M).astype(f),
        "expert_before": np.broadcast_to((np.arange(E) < np.arange(E)[:, None]).astype(f), (P, T, E, E)).copy(),
        "expert_rows": expert_rows,
        "own_block": np.broadcast_to(np.eye(M, dtype=f), (P, M, M)).copy(),
        "head_mask": (p[:, None] // HD == np.arange(H)).astype(f),
        "query_rows": (np.arange(M * M)[:, None] // M == np.arange(N) // BS).astype(f),
        "key_rows": (np.arange(M * M)[:, None] % M == np.arange(N) // BS).astype(f),
    }


def kernel(**inputs):
    import concourse.bacc as bacc
    from concourse.bass_utils import run_bass_kernel_spmd

    a = {k: np.ascontiguousarray(v) for k, v in inputs.items()}
    arrays = {
        "x": a["L0_attn_x"],
        "wqkv_t": np.ascontiguousarray(a["L0_attn_qkv_w"].T),
        "wproj_t": np.ascontiguousarray(a["L0_attn_proj_w"].T),
        "proj_b": np.ascontiguousarray(np.broadcast_to(a["L0_attn_proj_b"], (P, D))),
        "w1": a["L0_ffn_w1"],
        "b1_t": np.ascontiguousarray(a["L0_ffn_b1"].reshape(E * C, P).T),
        "w2": a["L0_ffn_w2"],
        "b2": a["L0_ffn_b2"],
        "wr": a["L0_ffn_wr"],
        "br": np.ascontiguousarray(np.broadcast_to(a["L0_ffn_br"], (P, E))),
    } | constants()
    nc = bacc.Bacc("TRN2", target_bir_lowering=False, num_devices=1)
    args = {k: nc.dram_tensor(f"in_{k}", v.shape, mybir.dt.from_np(v.dtype), kind="ExternalInput").ap()
            for k, v in arrays.items()}
    out = nc.dram_tensor("out_x", (B, N, D), F32, kind="ExternalOutput").ap()
    layer(nc, **args, out=out)
    r = run_bass_kernel_spmd(nc, [{f"in_{k}": v for k, v in arrays.items()}], core_ids=[0])
    return r.results[0]["out_x"]
```
